# Optimizing a Trainium2 kernel written in Bass

```python
import numpy as np
import jax
import jax.numpy as jnp

def _softmax(x, axis=-1):
    return jax.nn.softmax(x, axis=axis)
def _gelu(x):
    return jax.nn.gelu(x, approximate=True)
def _silu(x):
    return jax.nn.silu(x)
def _sigmoid(x):
    return jax.nn.sigmoid(x)
def _layernorm(x, axis=-1, eps=1e-5):
    m = jnp.mean(x, axis=axis, keepdims=True)
    v = jnp.var(x, axis=axis, keepdims=True)
    return (x - m) / jnp.sqrt(v + eps)
def _scatter_add(tgt, idx, src, axis=0):
    return tgt.at[idx].add(src)
def _segment_sum(src, seg, n):
    return jax.ops.segment_sum(src, seg, n)

kernel_name = 'mk_conv_seq_d1_conv_nchw512_12d9b1'

def setup_inputs(seed: int = 0):
    np.random.seed(seed)
    _w = jnp.asarray
    def _rec_inputs():
        import jax
        import jax.numpy as jnp
        _gk = jax.random.key(seed)
        x = 7.22e-05 + 1 * jax.random.normal(jax.random.fold_in(_gk, 1), (16, 512, 32, 32), jnp.float32)
        return x
    x = _rec_inputs()
    def _L0_conv_setup():
        import jax, jax.numpy as jnp
        import numpy as np
        NUM_GROUPS = 32
        NUM_HEADS = 8
        EPS = 1e-05

        def _group_norm(x, w, b):
            B, C, L = x.shape
            g = NUM_GROUPS
            xg = x.reshape(B, g, C // g, L)
            mean = jnp.mean(xg, axis=(2, 3), keepdims=True)
            var = jnp.var(xg, axis=(2, 3), keepdims=True)
            xn = ((xg - mean) * jax.lax.rsqrt(var + EPS)).reshape(B, C, L)
            return xn * w[None, :, None] + b[None, :, None]
        key = jax.random.key(seed)
        ks = jax.random.split(key, 4)
        b, c, h, w = (16, 512, 32, 32)
        x = jax.random.normal(ks[0], (b, c, h, w), dtype=jnp.float32)
        gn_w = jnp.ones((c,), dtype=jnp.float32)
        gn_b = jnp.zeros((c,), dtype=jnp.float32)
        qkv_w = jax.random.normal(ks[1], (3 * c, c), dtype=jnp.float32) * (1.0 / np.sqrt(c))
        qkv_b = jnp.zeros((3 * c,), dtype=jnp.float32)
        proj_w = jax.random.normal(ks[2], (c, c), dtype=jnp.float32) * (1.0 / np.sqrt(c))
        proj_b = jnp.zeros((c,), dtype=jnp.float32)
        return {'x': x, 'gn_w': gn_w, 'gn_b': gn_b, 'qkv_w': qkv_w, 'qkv_b': qkv_b, 'proj_w': proj_w, 'proj_b': proj_b}
    _L0_conv_all = _L0_conv_setup()
    _L0_conv_in = {k: v for k, v in _L0_conv_all.items() if k in ('gn_w', 'gn_b', 'qkv_w', 'qkv_b', 'proj_w', 'proj_b', )}
    del _L0_conv_all

    return {
        "x": x,
        "L0_conv_gn_w": _L0_conv_in["gn_w"],
        "L0_conv_gn_b": _L0_conv_in["gn_b"],
        "L0_conv_qkv_w": _L0_conv_in["qkv_w"],
        "L0_conv_qkv_b": _L0_conv_in["qkv_b"],
        "L0_conv_proj_w": _L0_conv_in["proj_w"],
        "L0_conv_proj_b": _L0_conv_in["proj_b"],
    }

def reference(x, L0_conv_gn_w, L0_conv_gn_b, L0_conv_qkv_w, L0_conv_qkv_b, L0_conv_proj_w, L0_conv_proj_b):
    import jax
    import jax.numpy as jnp
    def _L0_conv_ref(x, gn_w, gn_b, qkv_w, qkv_b, proj_w, proj_b):
        import jax, jax.numpy as jnp
        import numpy as np
        NUM_GROUPS = 32
        NUM_HEADS = 8
        EPS = 1e-05

        def _group_norm(x, w, b):
            B, C, L = x.shape
            g = NUM_GROUPS
            xg = x.reshape(B, g, C // g, L)
            mean = jnp.mean(xg, axis=(2, 3), keepdims=True)
            var = jnp.var(xg, axis=(2, 3), keepdims=True)
            xn = ((xg - mean) * jax.lax.rsqrt(var + EPS)).reshape(B, C, L)
            return xn * w[None, :, None] + b[None, :, None]
        b, c, h, w = x.shape
        L = h * w
        xr = x.reshape(b, c, L)
        xn = _group_norm(xr, gn_w, gn_b)
        qkv = jnp.einsum('oc,bcl->bol', qkv_w, xn) + qkv_b[None, :, None]
        q, k, v = jnp.split(qkv, 3, axis=1)
        H = NUM_HEADS
        ch = c // H
        bs = b * H
        q = q.reshape(bs, ch, L)
        k = k.reshape(bs, ch, L)
        v = v.reshape(bs, ch, L)
        scale = 1.0 / np.sqrt(np.sqrt(ch))
        weight = jnp.einsum('bct,bcs->bts', q * scale, k * scale)
        weight = jax.nn.softmax(weight.astype(jnp.float32), axis=-1).astype(weight.dtype)
        a = jnp.einsum('bts,bcs->bct', weight, v)
        a = a.reshape(b, c, L)
        a = jnp.einsum('oc,bcl->bol', proj_w, a) + proj_b[None, :, None]
        return (xr + a).reshape(b, c, h, w)

    def _gn(v, G=32, eps=1e-5):
        B_, C_, H_, W_ = v.shape
        g = v.reshape(B_, G, C_ // G, H_, W_)
        m = jnp.mean(g, axis=(2, 3, 4), keepdims=True)
        s = jnp.var(g, axis=(2, 3, 4), keepdims=True)
        return ((g - m) / jnp.sqrt(s + eps)).reshape(v.shape)

    def _ln_c(v, eps=1e-6):
        m = jnp.mean(v, axis=1, keepdims=True)
        s = jnp.var(v, axis=1, keepdims=True)
        return (v - m) / jnp.sqrt(s + eps)

    def _ln_t(v, eps=1e-5):
        m = jnp.mean(v, axis=-1, keepdims=True)
        s = jnp.var(v, axis=-1, keepdims=True)
        return (v - m) / jnp.sqrt(s + eps)

    def _to_tokens(v):
        B_, C_, H_, W_ = v.shape
        return v.reshape(B_, C_, H_ * W_).transpose(0, 2, 1)
    def _from_tokens(t, like):
        B_, C_, H_, W_ = like.shape
        return t.transpose(0, 2, 1).reshape(B_, C_, H_, W_)

    x = _L0_conv_ref(x, L0_conv_gn_w, L0_conv_gn_b, L0_conv_qkv_w, L0_conv_qkv_b, L0_conv_proj_w, L0_conv_proj_b)
    return x


_drawn_inputs = setup_inputs


def setup_inputs(seed=0):
    import zlib

    import numpy as np

    out = dict(_drawn_inputs(seed))
    spreads = {'L0_conv_gn_w': (1.0, 0.6),
     'L0_conv_gn_b': (0.0, 0.1),
     'L0_conv_qkv_b': (0.0, 0.1),
     'L0_conv_proj_b': (0.0, 0.1)}
    factors = {}
    for name, (base, spread) in spreads.items():
        noise = np.random.default_rng([zlib.crc32(name.encode()), seed]).standard_normal(out[name].shape)
        drawn = base * np.exp(spread * noise) if base else spread * noise
        out[name] = jnp.asarray(drawn.astype(out[name].dtype))
    for name, factor in factors.items():
        out[name] = (out[name] * factor).astype(out[name].dtype)
    return out
```

```python
from contextlib import ExitStack

import concourse.bass as bass
import concourse.mybir as mybir

F32 = mybir.dt.float32
F32R = mybir.dt.float32r
ALU = mybir.AluOpType
ACT = mybir.ActivationFunctionType
AX = mybir.AxisListType

P = 128
B, C, L = 16, 512, 1024
HEADS, GROUPS = 8, 32
CH = C // HEADS
CT = C // P
PAIRS = HEADS // 2
ST = L // P
HALF = 512
TC = L // HALF
ITEMS = 2 * ST
CHUNKS = ITEMS // 4
CQ = L // CHUNKS
EPS = 1e-5
QUARTERS = 4
QSCALE = 1.0 / CH ** 0.5

ACC_PROLOGUE = 2 + ST + 2 * TC
ACC_STEP = CHUNKS + 2 * TC
PROJ_GROUPS = CT * TC
ACC_TURN = 2 + ST + PROJ_GROUPS
STAT_LINKS = 10


def build(nc, x, w_qkv_t, w_proj_t, b_qkv, b_v_row, b_proj, gn_w, gn_b, ident_in, group_in, out):
    ctx = ExitStack()
    with ctx:
        def sb(name, shape, dt=F32):
            return ctx.enter_context(nc.sbuf_tensor(name, shape, dt))

        def ps(name, shape):
            return ctx.enter_context(nc.psum_tensor(name, shape, F32))

        def sem(name):
            return ctx.enter_context(nc.semaphore(name))

        w_v = sb("w_v", [P, 2, CT, C], F32R)
        w_o = sb("w_o", [P, CT, C])
        w_qk = sb("w_qk", [P, 2, CT, 2, P], F32R)
        x_img = sb("x_img", [P, CT, L])
        xn = sb("xn", [P, 2, CT, L], F32R)
        q_stack = sb("q_stack", [P, 2, L], F32R)
        k_stack = sb("k_stack", [P, 2, 2, L], F32R)
        v_img = sb("v_img", [P, ST, C])
        v_pair = sb("v_pair", [P, ST, P])
        probs = sb("probs", [P, 2, L])
        probs_t = sb("probs_t", [P, 2, 2, ST, CQ])
        attn = sb("attn", [P, PAIRS * L])
        part = sb("part", [P, 2, 2, HALF], F32R)
        resid = sb("resid", [P, 2, HALF])
        done = sb("done", [P, 2, HALF])
        bias_qkv = sb("bias_qkv", [P, 3 * CT])
        bias_qk = sb("bias_qk", [P, 2, PAIRS])
        bias_pair = sb("bias_pair", [P, 2])
        bias_v = sb("bias_v", [P, C])
        bias_o = sb("bias_o", [P, CT])
        gamma = sb("gamma", [P, CT])
        beta = sb("beta", [P, CT])
        ident = sb("ident", [P, P])
        group = sb("group", [P, P])
        neg_max = sb("neg_max", [P, ITEMS])
        row_sum = sb("row_sum", [P, ITEMS])
        row_inv = sb("row_inv", [P, ITEMS])
        bn = sb("bn", [P, CT, 2, 6])
        sum_means = sb("sum_means", [P, CT])
        dist = sb("dist", [P, CT * QUARTERS])
        dist_sq = sb("dist_sq", [P, CT * QUARTERS])
        mean_g = sb("mean_g", [P, CT])
        spread = sb("spread", [P, CT])
        var_g = sb("var_g", [P, CT])
        root = sb("root", [P, CT])
        rstd = sb("rstd", [P, CT])
        newton = sb("newton", [P, CT])
        scale_c = sb("scale_c", [P, CT])
        shift_c = sb("shift_c", [P, CT])

        scores = ps("scores", [P, 2, L])
        turned = ps("turned", [P, 2, 4, P])
        acc = ps("acc", [P, 2, HALF])

        w_qk_dram = nc.dram_tensor("w_qk_dram", [PAIRS, P, 2, CT, 2, P], F32R, kind="Internal").ap()

        consts_loaded = sem("consts_loaded")
        w_loaded = sem("w_loaded")
        w_hi_ready = sem("w_hi_ready")
        w_lo_ready = sem("w_lo_ready")
        w_stored = sem("w_stored")
        bias_ready = sem("bias_ready")
        pair_bias_ready = sem("pair_bias_ready")
        w_qk_loaded = sem("w_qk_loaded")
        x_loaded = sem("x_loaded")
        stat_link = sem("stat_link")
        root_ready = sem("root_ready")
        affine_step = sem("affine_step")
        affine_ready = sem("affine_ready")
        xn_hi_ready = sem("xn_hi_ready")
        xn_ready = sem("xn_ready")
        acc_filled = sem("acc_filled")
        acc_free = sem("acc_free")
        part_hi_ready = sem("part_hi_ready")
        stacked = [sem(f"stacked_{n}") for n in ("k0", "k1", "q0", "q1")]
        v_pair_loaded = sem("v_pair_loaded")
        scores_ready = sem("scores_ready")
        max_ready = sem("max_ready")
        exp_done = sem("exp_done")
        inv_ready = sem("inv_ready")
        probs_ready = sem("probs_ready")
        transposed = sem("transposed")
        probs_t_ready = sem("probs_t_ready")
        resid_loaded = [sem(f"resid_loaded_{n}") for n in range(2)]
        done_free = [sem(f"done_free_{n}") for n in range(2)]

        QK_GROUPS = [(1, 0), (1, 1), (0, 0), (0, 1)]

        def acc_base(b, j):
            return (b * PAIRS + j) * ACC_STEP + b * ACC_TURN + ACC_PROLOGUE

        def use_chunk(kind, c):
            return c + (2 if kind == "turn" and c else 0) + (2 * TC if kind != "end" and c == CHUNKS - 1 else 0)

        def use_average(n):
            return 1 + n

        def use_qk(kind, i):
            return CHUNKS - 1 + (2 if kind == "turn" else 0) + i

        def use_v(st):
            return ACC_STEP + 2 + st

        def use_out(kind, n):
            return (ACC_STEP + 2 + ST if kind == "turn" else CHUNKS) + n

        def half(tc):
            return slice(tc * HALF, (tc + 1) * HALF)

        block = ctx.enter_context(nc.Block())

        def load_w_qk(sp, j):
            sp.dma_start(w_qk[:].bitcast(F32).rearrange("p s c g o -> p (s c g o)"),
                         w_qk_dram[j].bitcast(F32).rearrange("p s c g o -> p (s c g o)")).then_inc(w_qk_loaded, 16)

        def stack_qk(sp, n, use, first=False):
            src = part[:].bitcast(F32)
            for i, (which, tc) in enumerate(QK_GROUPS):
                sp.wait_ge(acc_free, use + (i + 1))
                if i == 0 and not first:
                    sp.wait_ge(scores_ready, n * ITEMS)
                for h in range(2):
                    rows = slice(h * CH, (h + 1) * CH)
                    for s in range(2):
                        to = slice(s * CH, (s + 1) * CH)
                        if which:
                            sp.dma_start(k_stack[:].bitcast(F32)[to, h, :, half(tc)],
                                         src[rows, i % 2, :, :]).then_inc(stacked[i], 16)
                        else:
                            sp.dma_start(q_stack[:].bitcast(F32)[to, h, half(tc)],
                                         src[rows, i % 2, s, :]).then_inc(stacked[i], 16)

        def sync_step(sp, b, j, kind):
            g = b * PAIRS + j
            base = acc_base(b, j)
            sp.wait_ge(acc_free, base)
            sp.dma_start(v_pair[:], v_img[:, :, bass.ds(j * P, P)]).then_inc(v_pair_loaded, 16)
            if kind != "end":
                load_w_qk(sp, j + 1 if kind == "middle" else 0)
                stack_qk(sp, g + 1, base + use_qk(kind, 0))
            if kind == "middle":
                return
            for n in range(PROJ_GROUPS + 1):
                if n < PROJ_GROUPS:
                    if n >= 2:
                        sp.wait_ge(acc_free, base + (use_out(kind, n - 2) + 1))
                    ot, tc = divmod(n, TC)
                    sp.dma_start(resid[:, n % 2, :], x[b, ot * P:(ot + 1) * P, half(tc)])\
                      .then_inc(resid_loaded[n % 2], 16)
                if n:
                    sp.wait_ge(acc_free, base + (use_out(kind, n - 1) + 1))
                    ot, tc = divmod(n - 1, TC)
                    sp.dma_start(out[b, ot * P:(ot + 1) * P, half(tc)], done[:, (n - 1) % 2, :])\
                      .then_inc(done_free[(n - 1) % 2], 16)
        @block.sync
        def _(sp):
            for n in range(2):
                sp.sem_inc(done_free[n], 16)
            for dst, src in ((bias_qkv, b_qkv), (bias_v, b_v_row), (bias_o, b_proj), (gamma, gn_w), (beta, gn_b),
                             (ident, ident_in), (group, group_in)):
                sp.dma_start(dst[:], src).then_inc(consts_loaded, 16)
            sp.dma_start(x_img[:], x[0].rearrange("(c p) l -> p c l", p=P)).then_inc(x_loaded, 16)
            w_raw = probs_t[:].rearrange("p a h s q -> p (a h s q)")[:, 0:CT * 3 * C].rearrange("p (c o) -> p c o", c=CT)
            sp.dma_start(w_raw, w_qkv_t.rearrange("(c p) o -> p c o", p=P)).then_inc(w_loaded, 16)
            sp.dma_start(w_o[:], w_proj_t.rearrange("(c p) o -> p c o", p=P)).then_inc(consts_loaded, 16)
            sp.wait_ge(w_lo_ready, 3)
            split = xn[:].bitcast(F32).rearrange("p s c (g o) -> p (s c g) o", g=2)
            for j in range(PAIRS):
                sp.dma_start(w_qk_dram[j].bitcast(F32).rearrange("p s c g o -> p (s c g) o"),
                             split[:, :, j * P:(j + 1) * P]).then_inc(w_stored, 16)
            sp.wait_ge(w_stored, 16 * PAIRS)
            load_w_qk(sp, 0)
            stack_qk(sp, 0, ACC_PROLOGUE - 4, first=True)

            with sp.Fori(0, B - 1) as b:
                sp.wait_ge(xn_ready, (b + 1) * CT)
                sp.dma_start(x_img[:], x[b + 1].rearrange("(c p) l -> p c l", p=P)).then_inc(x_loaded, 16)
                with sp.Fori(0, PAIRS - 1) as j:
                    sync_step(sp, b, j, "middle")
                sync_step(sp, b, PAIRS - 1, "turn")
            with sp.Fori(0, PAIRS - 1) as j:
                sync_step(sp, B - 1, j, "middle")
            sync_step(sp, B - 1, PAIRS - 1, "end")
            for n in range(2):
                sp.wait_ge(done_free[n], 16 * (B * PROJ_GROUPS // 2 + 1))

        def split_lo(pool, b):
            for c in range(CT):
                pool.wait_ge(xn_hi_ready, b * CT + (c + 1))
                pool.tensor_tensor(xn[:, 1, c, :], x_img[:, c, :], xn[:, 0, c, :].bitcast(F32), ALU.subtract)\
                    .then_inc(xn_ready, 1)

        @block.gpsimd
        def _(pool):
            split_lo(pool, 0)
            with pool.Fori(1, B) as b:
                split_lo(pool, b)

        def group_root(act, b, use):
            act.wait_ge(acc_free, use + 1)
            nc.scalar.activation(root[:], var_g[:], ACT.Sqrt).then_inc(root_ready, 1)

        def normalise(act, b, c):
            act.wait_ge(affine_ready, b + 1)
            nc.scalar.activation(xn[:, 0, c, :], x_img[:, c, :], ACT.Identity,
                                 bias=shift_c[:, c:c + 1], scale=scale_c[:, c:c + 1])
            nc.scalar.activation(x_img[:, c, :], x_img[:, c, :], ACT.Identity,
                                 bias=shift_c[:, c:c + 1], scale=scale_c[:, c:c + 1]).then_inc(xn_hi_ready, 1)

        def part_hi(act, n, i, use, bank, first=False):
            which, _ = QK_GROUPS[i]
            act.wait_ge(acc_filled, use + 1)
            if i >= 2 or not first:
                act.wait_ge(stacked[(i + 2) % 4], (n if i < 2 else n + 1) * 64)
            if i == 0:
                act.wait_ge(pair_bias_ready, n + 1)
            nc.scalar.activation(part[:, i % 2, 0, :], acc[:, bank, :], ACT.Identity,
                                 bias=bias_pair[:, which:which + 1]).then_inc(part_hi_ready, 1)

        def softmax_exp(act, g, i, first=False):
            act.wait_ge(max_ready, g * ITEMS + (i + 1))
            if not first:
                act.wait_ge(transposed, g * 2 * ITEMS + (2 * (i - 1) if i >= 2 else 0))
            nc.scalar.activation(probs[:, i % 2, :], scores[:, i % 2, :], ACT.Exp, bias=neg_max[:, i:i + 1],
                                 accum_out=row_sum[:, i:i + 1]).then_inc(exp_done, 1)

        def copy_turned(act, b, j, kind, i):
            g = b * PAIRS + j
            c, h, t = i // 4, i % 2, i // 2 % 2
            if i == 0:
                act.wait_ge(acc_filled, acc_base(b, j))
            elif i % 4 == 0 and c >= 2:
                act.wait_ge(acc_filled, acc_base(b, j) + (use_chunk(kind, c - 2) + 1))
            for k in range(2):
                act.wait_ge(transposed, g * 2 * ITEMS + (2 * i + k + 1))
                nc.scalar.activation(probs_t[:, c % 2, h, 4 * k:4 * k + 4, t * P:(t + 1) * P], turned[:, k, :, :],
                                     ACT.Copy).then_inc(probs_t_ready, 1)

        def scalar_step(act, b, j, kind):
            g = b * PAIRS + j
            base = acc_base(b, j)
            for i in range(ITEMS - 2):
                copy_turned(act, b, j, kind, i)
                softmax_exp(act, g, i + 2)
                if kind == "turn" and i == 6:
                    group_root(act, b + 1, base + use_average(1))
                if kind == "turn" and i >= 7 and i % 2:
                    if i == 7:
                        act.wait_ge(acc_filled, base)
                    normalise(act, b + 1, (i - 7) // 2)
            if kind != "end":
                for i in range(3):
                    part_hi(act, g + 1, i, base + use_qk(kind, i), (i + 1) % 2)
            copy_turned(act, b, j, kind, ITEMS - 2)
            copy_turned(act, b, j, kind, ITEMS - 1)
            if kind != "end":
                part_hi(act, g + 1, 3, base + use_qk(kind, 3), 0)
                softmax_exp(act, g + 1, 0)
                softmax_exp(act, g + 1, 1)

        @block.scalar
        def _(act):
            w_raw = probs_t[:].rearrange("p a h s q -> p (a h s q)")[:, 0:CT * 3 * C].rearrange("p (c o) -> p c o", c=CT)
            act.wait_ge(w_loaded, 16)
            nc.scalar.activation(xn[:, 0, :, 0:C], w_raw[:, :, 0:C], ACT.Copy, scale=QSCALE).then_inc(w_hi_ready, 1)
            nc.scalar.activation(xn[:, 0, :, C:2 * C], w_raw[:, :, C:2 * C], ACT.Copy).then_inc(w_hi_ready, 1)
            nc.scalar.activation(w_v[:, 0, :, :], w_raw[:, :, 2 * C:3 * C], ACT.Copy).then_inc(w_hi_ready, 1)
            act.wait_ge(w_stored, 16 * PAIRS)
            group_root(act, 0, 1)
            for c in range(CT):
                normalise(act, 0, c)
            for i in range(4):
                part_hi(act, 0, i, ACC_PROLOGUE - 4 + i, i % 2, first=True)
            softmax_exp(act, 0, 0, first=True)
            softmax_exp(act, 0, 1, first=True)

            with act.Fori(0, B - 1) as b:
                with act.Fori(0, PAIRS - 1) as j:
                    scalar_step(act, b, j, "middle")
                scalar_step(act, b, PAIRS - 1, "turn")
            with act.Fori(0, PAIRS - 1) as j:
                scalar_step(act, B - 1, j, "middle")
            scalar_step(act, B - 1, PAIRS - 1, "end")

        def channel_stats(dve, b, n):
            c, h = divmod(n, 2)
            if n == 0:
                dve.wait_ge(x_loaded, (b + 1) * 16)
            last = nc.vector.bn_stats(bn[:, c, h, :], x_img[:, c, half(h)])
            if n == 2 * CT - 1:
                last.then_inc(stat_link, 1)

        def sum_of_means(dve, b):
            dve.wait_ge(stat_link, b * STAT_LINKS + 1)
            nc.vector.tensor_reduce(sum_means[:], quarter(1).rearrange("p (c q) -> p c q", q=QUARTERS), AX.X, ALU.add)\
              .then_inc(stat_link, 1)

        def quarter(field):
            return bn[:].rearrange("p c h (e f) -> p (c h e) f", f=3)[:, :, field]

        def group_mean(dve, b, use, slot):
            base = b * STAT_LINKS
            dve.wait_ge(acc_filled, use + 1)
            nc.vector.tensor_scalar(mean_g[:], acc[:, slot, 0:CT], 1.0 / QUARTERS, None, ALU.mult).then_inc(acc_free, 1)
            dve.wait_ge(acc_free, use + 1)
            for c in range(CT):
                q = slice(c * QUARTERS, (c + 1) * QUARTERS)
                last = nc.vector.tensor_scalar(dist[:, q], quarter(1)[:, q], mean_g[:, c:c + 1], None, ALU.subtract)
            last.then_inc(stat_link, 1)
            dve.wait_ge(stat_link, base + 3)
            nc.vector.tensor_tensor(dist_sq[:], dist[:], dist[:], ALU.mult).then_inc(stat_link, 1)
            dve.wait_ge(stat_link, base + 4)
            nc.vector.scalar_tensor_tensor(dist[:], quarter(2), 1.0 * QUARTERS / L, dist_sq[:], ALU.mult, ALU.add)\
              .then_inc(stat_link, 1)
            dve.wait_ge(stat_link, base + 5)
            nc.vector.tensor_reduce(spread[:], dist[:].rearrange("p (c q) -> p c q", q=QUARTERS), AX.X, ALU.add)\
              .then_inc(stat_link, 1)

        def group_variance(dve, b, use, slot):
            dve.wait_ge(acc_filled, use + 1)
            nc.vector.tensor_scalar(var_g[:], acc[:, slot, 0:CT], 1.0 / QUARTERS, EPS, ALU.mult, ALU.add).then_inc(acc_free, 1)

        def group_affine(dve, b):
            base = b * STAT_LINKS
            dve.wait_ge(root_ready, b + 1)
            nc.vector.reciprocal(rstd[:], root[:]).then_inc(stat_link, 1)
            dve.wait_ge(stat_link, base + 7)
            nc.vector.tensor_tensor(newton[:], rstd[:], rstd[:], ALU.mult).then_inc(stat_link, 1)
            dve.wait_ge(stat_link, base + 8)
            nc.vector.scalar_tensor_tensor(newton[:], newton[:], -0.5, var_g[:], ALU.mult, ALU.mult)\
              .then_inc(stat_link, 1)
            dve.wait_ge(stat_link, base + 9)
            nc.vector.scalar_tensor_tensor(rstd[:], newton[:], 1.5, rstd[:], ALU.add, ALU.mult).then_inc(stat_link, 1)
            dve.wait_ge(stat_link, base + 10)
            nc.vector.tensor_tensor(scale_c[:], rstd[:], gamma[:], ALU.mult).then_inc(affine_step, 1)
            dve.wait_ge(affine_step, b * 2 + 1)
            nc.vector.tensor_tensor(newton[:], mean_g[:], scale_c[:], ALU.mult).then_inc(affine_step, 1)
            dve.wait_ge(affine_step, b * 2 + 2)
            nc.vector.tensor_tensor(shift_c[:], beta[:], newton[:], ALU.subtract).then_inc(affine_ready, 1)

        def v_out(dve, b, st, use, first=False):
            dve.wait_ge(acc_filled, use + 1)
            if st == 0 and not first:
                dve.wait_ge(v_pair_loaded, b * PAIRS * 16)
            nc.vector.tensor_tensor(v_img[:, st, :], acc[:, st % 2, :], bias_v[:], ALU.add).then_inc(acc_free, 1)

        def pair_bias(dve, j):
            nc.vector.tensor_scalar(bias_pair[:].rearrange("p (k o) -> p k o", o=1), bias_qk[:, :, bass.ds(j, 1)], 1.0,
                                    None, ALU.mult).then_inc(pair_bias_ready, 1)

        def part_lo(dve, n, i, bank):
            which, _ = QK_GROUPS[i]
            dve.wait_ge(part_hi_ready, n * 4 + (i + 1))
            nc.vector.scalar_tensor_tensor(part[:, i % 2, 1, :], acc[:, bank, :],
                                           bias_pair[:, which:which + 1],
                                           part[:, i % 2, 0, :].bitcast(F32), ALU.add, ALU.subtract)\
              .then_inc(acc_free, 1)

        def row_max(dve, g, i):
            dve.wait_ge(scores_ready, g * ITEMS + (i + 1))
            nc.vector.tensor_reduce(neg_max[:, i:i + 1], scores[:, i % 2, :], AX.X, ALU.max, negate=True)\
              .then_inc(max_ready, 1)

        def divide(dve, g, i):
            dve.wait_ge(exp_done, g * ITEMS + (i + 1))
            nc.vector.reciprocal(row_inv[:, i:i + 1], row_sum[:, i:i + 1]).then_inc(inv_ready, 1)
            dve.wait_ge(inv_ready, g * ITEMS + (i + 1))
            nc.vector.tensor_scalar(probs[:, i % 2, :], probs[:, i % 2, :], row_inv[:, i:i + 1], None, ALU.mult)\
              .then_inc(probs_ready, 1)

        def attn_out(dve, j, c, use, slot):
            dve.wait_ge(acc_filled, use + 1)
            nc.vector.tensor_copy(attn[:, bass.ds(j * L + c * CQ, CQ)], acc[:, slot, 0:CQ]).then_inc(acc_free, 1)

        def proj_out(dve, b, n, use):
            ot = n // TC
            dve.wait_ge(acc_filled, use + 1)
            dve.wait_ge(resid_loaded[n % 2], (b * (PROJ_GROUPS // 2) + (n // 2 + 1)) * 16)
            dve.wait_ge(done_free[n % 2], (b * (PROJ_GROUPS // 2) + (n // 2 + 1)) * 16)
            nc.vector.scalar_tensor_tensor(done[:, n % 2, :], acc[:, n % 2, :], bias_o[:, ot:ot + 1],
                                           resid[:, n % 2, :], ALU.add, ALU.add).then_inc(acc_free, 1)

        def vector_step(dve, b, j, kind):
            g = b * PAIRS + j
            base = acc_base(b, j)
            if kind != "end":
                pair_bias(dve, j + 1 if kind == "middle" else 0)
            for i in range(ITEMS - 2):
                row_max(dve, g, i + 2)
                divide(dve, g, i + 1)
                if i in (5, 9, 13):
                    c = (i - 5) // 4
                    attn_out(dve, j, c, base + use_chunk(kind, c), c % 2)
                if kind == "turn":
                    if i < 4:
                        channel_stats(dve, b + 1, 2 * i)
                        channel_stats(dve, b + 1, 2 * i + 1)
                    elif i == 4:
                        sum_of_means(dve, b + 1)
                    elif i == 5:
                        group_mean(dve, b + 1, base + use_average(0), 1)
                    elif i == 6:
                        group_variance(dve, b + 1, base + use_average(1), 0)
                    elif i == 7:
                        group_affine(dve, b + 1)
            divide(dve, g, ITEMS - 1)
            if kind != "end":
                dve.wait_ge(pair_bias_ready, g + 2)
                for i in range(4):
                    part_lo(dve, g + 1, i, (i + 1) % 2)
                row_max(dve, g + 1, 0)
                row_max(dve, g + 1, 1)
                divide(dve, g + 1, 0)
            attn_out(dve, j, CHUNKS - 1, base + use_chunk(kind, CHUNKS - 1), 1)
            if kind == "turn":
                for st in range(ST):
                    v_out(dve, b + 1, st, base + use_v(st))
            if kind != "middle":
                for n in range(PROJ_GROUPS):
                    proj_out(dve, b, n, base + use_out(kind, n))

        @block.vector
        def _(dve):
            w_raw = probs_t[:].rearrange("p a h s q -> p (a h s q)")[:, 0:CT * 3 * C].rearrange("p (c o) -> p c o", c=CT)
            for n, (hi, lo, scale) in enumerate(((xn[:, 0, :, 0:C], xn[:, 1, :, 0:C], QSCALE),
                                                 (xn[:, 0, :, C:2 * C], xn[:, 1, :, C:2 * C], 1.0),
                                                 (w_v[:, 0, :, :], w_v[:, 1, :, :], 1.0))):
                dve.wait_ge(w_hi_ready, n + 1)
                nc.vector.scalar_tensor_tensor(lo, w_raw[:, :, n * C:(n + 1) * C], scale, hi.bitcast(F32),
                                               ALU.mult, ALU.subtract).then_inc(w_lo_ready, 1)
            dve.wait_ge(consts_loaded, 16 * 8)
            nc.vector.tensor_scalar(bias_qk[:, 0, :], bias_qkv[:, 0:CT], QSCALE, None, ALU.mult).then_inc(bias_ready, 1)
            nc.vector.tensor_copy(bias_qk[:, 1, :], bias_qkv[:, CT:2 * CT]).then_inc(bias_ready, 1)
            dve.wait_ge(bias_ready, 2)
            pair_bias(dve, 0)
            for n in range(2 * CT):
                channel_stats(dve, 0, n)
            sum_of_means(dve, 0)
            group_mean(dve, 0, 0, 0)
            group_variance(dve, 0, 1, 1)
            group_affine(dve, 0)
            for st in range(ST):
                v_out(dve, 0, st, 2 + st, first=True)
            dve.wait_ge(pair_bias_ready, 1)
            for i in range(4):
                part_lo(dve, 0, i, i % 2)
            row_max(dve, 0, 0)
            row_max(dve, 0, 1)
            divide(dve, 0, 0)

            with dve.Fori(0, B - 1) as b:
                with dve.Fori(0, PAIRS - 1) as j:
                    vector_step(dve, b, j, "middle")
                vector_step(dve, b, PAIRS - 1, "turn")
            with dve.Fori(0, PAIRS - 1) as j:
                vector_step(dve, B - 1, j, "middle")
            vector_step(dve, B - 1, PAIRS - 1, "end")

        def bank_free(pe, use, first=False):
            if not first:
                pe.wait_ge(acc_free, use - 1)

        def group_average(pe, b, which, use, bank, first=False):
            pe.wait_ge(stat_link, b * STAT_LINKS + (2, 6)[which])
            bank_free(pe, use, first)
            src = (sum_means, spread)[which][:]
            nc.tensor.matmul(acc[:, bank, 0:CT], group[:], src, start=True, stop=True).then_inc(acc_filled, 1)

        def split_product(terms, out_ap, inc):
            for n, (lhs, rhs) in enumerate(terms):
                last = nc.tensor.matmul(out_ap, lhs, rhs, start=n == 0, stop=n == len(terms) - 1)
            return last.then_inc(inc, 1)

        def project_v(pe, st, use):
            px = slice(st * P, (st + 1) * P)
            bank_free(pe, use)
            split_product([(xn[:, a, c, px], w_v[:, w, c, :]) for c in range(CT) for a, w in ((0, 0), (0, 1), (1, 0))],
                          acc[:, st % 2, :], acc_filled)

        def project_qk(pe, i, use, bank):
            which, tc = QK_GROUPS[i]
            bank_free(pe, use)
            split_product([(w_qk[:, w, c, which, :], xn[:, a, c, half(tc)])
                           for c in range(CT) for w, a in ((0, 0), (0, 1), (1, 0))], acc[:, bank, :], acc_filled)

        def score(pe, g, i, first=False):
            t, h = divmod(i, 2)
            if i == 0:
                for n in range(3):
                    pe.wait_ge(stacked[n], (g + 1) * 64)
            if i == ITEMS // 2:
                pe.wait_ge(stacked[3], (g + 1) * 64)
            if not first:
                pe.wait_ge(exp_done, g * ITEMS + (i - 1))
            lhs = q_stack[:, h, t * P:(t + 1) * P]
            for tc in range(TC):
                nc.tensor.matmul(scores[:, i % 2, half(tc)], lhs, k_stack[:, h, 0, half(tc)], start=True, stop=False)
                last = nc.tensor.matmul(scores[:, i % 2, half(tc)], lhs, k_stack[:, h, 1, half(tc)],
                                        start=False, stop=True)
            last.then_inc(scores_ready, 1)

        def transpose(pe, g, i):
            pe.wait_ge(probs_ready, g * ITEMS + (i + 1))
            for k in range(2):
                if i:
                    pe.wait_ge(probs_t_ready, g * 2 * ITEMS + (2 * i - 1 + k))
                for n in range(4):
                    s = (4 * k + n) * P
                    last = nc.tensor.transpose(turned[:, k, n, :], probs[:, i % 2, s:s + P], ident[:])
                last.then_inc(transposed, 1)

        def attend(pe, g, c, use, slot):
            pe.wait_ge(probs_t_ready, g * 2 * ITEMS + 8 * (c + 1))
            if c == 0:
                pe.wait_ge(v_pair_loaded, (g + 1) * 16)
            bank_free(pe, use)
            for st in range(ST):
                for h in range(2):
                    rows = slice(h * CH, (h + 1) * CH)
                    last = nc.tensor.matmul(acc[rows, slot, 0:CQ], v_pair[:, st, rows], probs_t[:, c % 2, h, st, :],
                                            start=st == 0, stop=st == ST - 1)
            last.then_inc(acc_filled, 1)

        def project_out(pe, n, use):
            ot, tc = divmod(n, TC)
            bank_free(pe, use)
            if n == 0:
                pe.wait_ge(acc_free, use)
            for c in range(CT):
                last = nc.tensor.matmul(acc[:, n % 2, :], w_o[:, c, ot * P:(ot + 1) * P], attn[:, c * L + tc * HALF:c * L + (tc + 1) * HALF],
                                        start=c == 0, stop=c == CT - 1)
            last.then_inc(acc_filled, 1)

        def tensor_step(pe, b, j, kind):
            g = b * PAIRS + j
            base = acc_base(b, j)
            for i in range(ITEMS - 2):
                score(pe, g, i + 2)
                transpose(pe, g, i)
                if i in (4, 8, 12):
                    c = i // 4 - 1
                    attend(pe, g, c, base + use_chunk(kind, c), c % 2)
                if kind == "turn" and i in (5, 6):
                    group_average(pe, b + 1, i - 5, base + use_average(i - 5), (1 + i - 5) % 2)
            if kind != "end":
                pe.wait_ge(w_qk_loaded, (g + 2) * 16)
                if kind == "turn":
                    pe.wait_ge(xn_ready, (b + 2) * CT)
                for i in range(3):
                    project_qk(pe, i, base + use_qk(kind, i), (i + 1) % 2)
            transpose(pe, g, ITEMS - 2)
            transpose(pe, g, ITEMS - 1)
            if kind != "end":
                project_qk(pe, 3, base + use_qk(kind, 3), 0)
                score(pe, g + 1, 0)
                score(pe, g + 1, 1)
            attend(pe, g, CHUNKS - 1, base + use_chunk(kind, CHUNKS - 1), 1)
            if kind == "turn":
                for st in range(ST):
                    project_v(pe, st, base + use_v(st))
            if kind != "middle":
                for n in range(PROJ_GROUPS):
                    project_out(pe, n, base + use_out(kind, n))

        @block.tensor
        def _(pe):
            pe.wait_ge(consts_loaded, 16 * 8)
            group_average(pe, 0, 0, 0, 0, first=True)
            group_average(pe, 0, 1, 1, 1, first=True)
            pe.wait_ge(w_lo_ready, 3)
            pe.wait_ge(xn_ready, CT)
            for st in range(ST):
                project_v(pe, st, 2 + st)
            pe.wait_ge(w_qk_loaded, 16)
            for i in range(4):
                project_qk(pe, i, 2 + ST + i, i % 2)
            score(pe, 0, 0, first=True)
            score(pe, 0, 1, first=True)

            with pe.Fori(0, B - 1) as b:
                with pe.Fori(0, PAIRS - 1) as j:
                    tensor_step(pe, b, j, "middle")
                tensor_step(pe, b, PAIRS - 1, "turn")
            with pe.Fori(0, PAIRS - 1) as j:
                tensor_step(pe, B - 1, j, "middle")
            tensor_step(pe, B - 1, PAIRS - 1, "end")

    return nc


def kernel(x, L0_conv_gn_w, L0_conv_gn_b, L0_conv_qkv_w, L0_conv_qkv_b, L0_conv_proj_w, L0_conv_proj_b):
    import numpy as np
    import concourse.bacc as bacc
    from concourse.bass_utils import run_bass_kernel_spmd

    def columns(a):
        return np.ascontiguousarray(np.asarray(a).reshape(-1, P).T)

    same_group = np.arange(P)[:, None] // (C // GROUPS) == np.arange(P)[None, :] // (C // GROUPS)
    arrays = {
        "x": np.ascontiguousarray(np.asarray(x).reshape(B, C, L)),
        "w_qkv_t": np.ascontiguousarray(np.asarray(L0_conv_qkv_w).T),
        "w_proj_t": np.ascontiguousarray(np.asarray(L0_conv_proj_w).T),
        "b_qkv": columns(L0_conv_qkv_b),
        "b_v_row": np.ascontiguousarray(np.broadcast_to(np.asarray(L0_conv_qkv_b)[None, 2 * C:], (P, C))),
        "b_proj": columns(L0_conv_proj_b),
        "gn_w": columns(L0_conv_gn_w),
        "gn_b": columns(L0_conv_gn_b),
        "identity": np.eye(P, dtype=np.float32),
        "group_mean": same_group.astype(np.float32) / np.float32(C // GROUPS),
    }
    nc = bacc.Bacc("TRN2", target_bir_lowering=False, num_devices=1)
    args = [nc.dram_tensor(n, a.shape, F32, kind="ExternalInput").ap() for n, a in arrays.items()]
    out = nc.dram_tensor("out", (B, C, L), F32, kind="ExternalOutput").ap()
    build(nc, *args, out)
    result = run_bass_kernel_spmd(nc, [arrays], core_ids=[0])
    return result.results[0]["out"].reshape(B, C, 32, 32)
```

```python
from contextlib import ExitStack

import concourse.bass as bass
import concourse.mybir as mybir

F32 = mybir.dt.float32
F32R = mybir.dt.float32r
ALU = mybir.AluOpType
ACT = mybir.ActivationFunctionType
AX = mybir.AxisListType

P = 128
B, C, L = 16, 512, 1024
HEADS, GROUPS = 8, 32
CH = C // HEADS
CT = C // P
PAIRS = HEADS // 2
ST = L // P
HALF = 512
TC = L // HALF
ITEMS = 2 * ST
CHUNKS = ITEMS // 4
CQ = L // CHUNKS
EPS = 1e-5
QUARTERS = 4
QSCALE = 1.0 / CH ** 0.5

ACC_PROLOGUE = 2 + ST + 3
ACC_STEP = CHUNKS + 2 * TC
PROJ_GROUPS = CT * TC
ACC_TURN = 2 + ST + PROJ_GROUPS
STAT_LINKS = 10


def build(nc, x, w_qkv_t, w_proj_t, b_qkv, b_v_row, b_proj, gn_w, gn_b, ident_in, group_in, out):
    ctx = ExitStack()
    with ctx:
        def sb(name, shape, dt=F32):
            return ctx.enter_context(nc.sbuf_tensor(name, shape, dt))

        def ps(name, shape):
            return ctx.enter_context(nc.psum_tensor(name, shape, F32))

        def sem(name):
            return ctx.enter_context(nc.semaphore(name))

        w_v = sb("w_v", [P, 2, CT, C], F32R)
        w_o = sb("w_o", [P, 2, CT, C], F32R)
        w_qk = sb("w_qk", [P, 2, CT, 2, P], F32R)
        x_img = sb("x_img", [P, CT * L])
        xn = sb("xn", [P, 2, CT, L], F32R)
        q_stack = sb("q_stack", [P, 2, L], F32R)
        k_stack = sb("k_stack", [P, 2, 2, L], F32R)
        v_img = sb("v_img", [P, ST, C])
        v_pair = sb("v_pair", [P, ST, P])
        probs = sb("probs", [P, 2, L])
        with nc.sbuf_tensor("attn_split", [P, 2, PAIRS, L], F32R) as attn_split:
            pass
        probs_t = sb("probs_t", [P, 2, 2, ST, CQ])
        attn = sb("attn", [P, PAIRS * L])
        resid = sb("resid", [P, 2, HALF])
        done = sb("done", [P, 2, HALF])
        bias_qkv = sb("bias_qkv", [P, 3 * CT])
        bias_qk = sb("bias_qk", [P, 2, PAIRS])
        bias_pair = sb("bias_pair", [P, 2])
        bias_v = sb("bias_v", [P, C])
        bias_o = sb("bias_o", [P, CT])
        gamma = sb("gamma", [P, CT])
        beta = sb("beta", [P, CT])
        ident = sb("ident", [P, P])
        group = sb("group", [P, P])
        neg_max = sb("neg_max", [P, ITEMS])
        row_sum = sb("row_sum", [P, ITEMS])
        row_inv = sb("row_inv", [P, ITEMS])
        bn = sb("bn", [P, CT * 2 * 6])
        sum_means = sb("sum_means", [P, CT])
        dist = sb("dist", [P, CT * QUARTERS])
        dist_sq = sb("dist_sq", [P, CT * QUARTERS])
        mean_g = sb("mean_g", [P, CT])
        spread = sb("spread", [P, CT])
        var_g = sb("var_g", [P, CT])
        root = sb("root", [P, CT])
        rstd = sb("rstd", [P, CT])
        newton = sb("newton", [P, CT])
        scale_c = sb("scale_c", [P, CT])
        shift_c = sb("shift_c", [P, CT])

        scores = ps("scores", [P, 2, L])
        turned = ps("turned", [P, 2, 4, P])
        acc = ps("acc", [P, 2, HALF])

        w_qk_dram = nc.dram_tensor("w_qk_dram", [PAIRS, P, 2, CT, 2, P], F32R, kind="Internal").ap()

        consts_loaded = sem("consts_loaded")
        group_loaded = sem("group_loaded")
        w_v_loaded = sem("w_v_loaded")
        w_qk_raw_loaded = sem("w_qk_raw_loaded")
        w_o_loaded = sem("w_o_loaded")
        w_hi_ready = sem("w_hi_ready")
        w_lo_ready = sem("w_lo_ready")
        w_stored = sem("w_stored")
        bias_ready = sem("bias_ready")
        pair_bias_ready = sem("pair_bias_ready")
        w_qk_loaded = sem("w_qk_loaded")
        first_x_loaded = sem("first_x_loaded")
        x_loaded = sem("x_loaded")
        stat_link = sem("stat_link")
        root_ready = sem("root_ready")
        affine_step = sem("affine_step")
        affine_ready = sem("affine_ready")
        xn_hi_ready = sem("xn_hi_ready")
        xn_full_ready = sem("xn_full_ready")
        xn_ready = sem("xn_ready")
        acc_filled = sem("acc_filled")
        acc_free = sem("acc_free")
        qk_hi_ready = sem("qk_hi_ready")
        v_pair_loaded = sem("v_pair_loaded")
        scores_ready = sem("scores_ready")
        max_ready = sem("max_ready")
        exp_done = sem("exp_done")
        inv_ready = sem("inv_ready")
        probs_ready = sem("probs_ready")
        transposed = sem("transposed")
        probs_t_ready = sem("probs_t_ready")
        attn_hi_ready = sem("attn_hi_ready")
        attn_lo_ready = sem("attn_lo_ready")
        resid_loaded = [sem(f"resid_loaded_{n}") for n in range(2)]
        done_free = [sem(f"done_free_{n}") for n in range(2)]

        QK_GROUPS = [(1, 0), (1, 1), (0, 0), (0, 1)]

        def acc_base(b, j):
            return (b * PAIRS + j) * ACC_STEP + b * ACC_TURN + ACC_PROLOGUE

        def bank(use):
            return (ACC_PROLOGUE + use) % 2

        USE_LAST_QK = 0
        USE_AVERAGE = 1

        def use_chunk(kind, c):
            return 1 + (2 if kind == "turn" else 0) + c + (3 if kind != "end" and c == CHUNKS - 1 else 0)

        def use_qk(kind, i):
            return use_chunk(kind, CHUNKS - 2) + 1 + i

        def use_v(st):
            return ACC_STEP + 2 + st

        def use_out(kind, n):
            return (ACC_STEP + 2 + ST if kind == "turn" else 1 + CHUNKS) + n

        def half(tc):
            return slice(tc * HALF, (tc + 1) * HALF)

        def tile_of(c):
            return x_img[:, c * L:(c + 1) * L]

        probs_t_flat = probs_t[:].rearrange("p a h s q -> p (a h s q)")
        w_raw = probs_t_flat[:, 0:CT * 3 * C].rearrange("p (c o) -> p c o", c=CT)
        w_o_raw = probs_t_flat[:, CT * 3 * C:CT * 4 * C].rearrange("p (c o) -> p c o", c=CT)
        q_parts = k_stack[:].rearrange("p h s (c l) -> p (h s c l)", l=C).rearrange("p (s c o) -> p s c o", s=2, c=CT)
        split_parts = ((q_parts[:, 0], q_parts[:, 1]),
                       (q_stack[:].rearrange("p h l -> p (h l)").rearrange("p (c o) -> p c o", c=CT),
                        w_qk[:].rearrange("p s c g o -> p (s c g o)").rearrange("p (c o) -> p c o", c=CT)))

        block = ctx.enter_context(nc.Block())

        def load_image(queue, b, loaded):
            queue.dma_start(x_img[:].rearrange("p (c l) -> p c l", c=CT),
                         x[b].rearrange("(c p) l -> p c l", p=P)).then_inc(loaded, 16)

        def load_w_qk(sp, j):
            sp.dma_start(w_qk[:].bitcast(F32).rearrange("p s c g o -> p (s c g o)"),
                         w_qk_dram[j].bitcast(F32).rearrange("p s c g o -> p (s c g o)")).then_inc(w_qk_loaded, 16)

        def sync_step(sp, b, j, kind):
            g = b * PAIRS + j
            base = acc_base(b, j)
            sp.wait_ge(acc_free, base)
            sp.dma_start(v_pair[:], v_img[:, :, bass.ds(j * P, P)]).then_inc(v_pair_loaded, 16)
            if kind != "end":
                sp.wait_ge(acc_free, base + (USE_LAST_QK + 1))
                load_w_qk(sp, j + 1 if kind == "middle" else 0)
            if kind == "middle":
                return
            for n in range(PROJ_GROUPS + 1):
                if n < PROJ_GROUPS:
                    if n >= 2:
                        sp.wait_ge(acc_free, base + (use_out(kind, n - 2) + 1))
                    ot, tc = divmod(n, TC)
                    sp.dma_start(resid[:, n % 2, :], x[b, ot * P:(ot + 1) * P, half(tc)])\
                      .then_inc(resid_loaded[n % 2], 16)
                if n:
                    sp.wait_ge(acc_free, base + (use_out(kind, n - 1) + 1))
                    ot, tc = divmod(n - 1, TC)
                    sp.dma_start(out[b, ot * P:(ot + 1) * P, half(tc)], done[:, (n - 1) % 2, :])\
                      .then_inc(done_free[(n - 1) % 2], 16)
        @block.sync
        def _(sp):
            for n in range(2):
                sp.sem_inc(done_free[n], 16)
            for dst, src in ((group, group_in), (gamma, gn_w), (beta, gn_b)):
                sp.dma_start(dst[:], src).then_inc(group_loaded, 16)
            load_image(sp, 0, first_x_loaded)
            w_rows = w_qkv_t.rearrange("(c p) o -> p c o", p=P)
            sp.dma_start(w_raw[:, :, 2 * C:3 * C], w_rows[:, :, 2 * C:3 * C]).then_inc(w_v_loaded, 16)
            sp.dma_start(w_raw[:, :, 0:2 * C], w_rows[:, :, 0:2 * C]).then_inc(w_qk_raw_loaded, 16)
            for dst, src in ((bias_qkv, b_qkv), (bias_v, b_v_row), (bias_o, b_proj), (ident, ident_in)):
                sp.dma_start(dst[:], src).then_inc(consts_loaded, 16)
            sp.dma_start(w_o_raw, w_proj_t.rearrange("(c p) o -> p c o", p=P)).then_inc(w_o_loaded, 16)
            sp.wait_ge(w_lo_ready, 3)
            for which in range(2):
                for part in range(2):
                    for j in range(PAIRS):
                        sp.dma_start(w_qk_dram[j, :, part, :, which, :].bitcast(F32),
                                     split_parts[which][part].bitcast(F32)[:, :, j * P:(j + 1) * P])\
                          .then_inc(w_stored, 16)
            sp.wait_ge(w_stored, 16 * 4 * PAIRS)
            load_w_qk(sp, 0)

            with sp.Fori(0, B - 1) as b:
                with sp.Fori(0, PAIRS - 1) as j:
                    sync_step(sp, b, j, "middle")
                sync_step(sp, b, PAIRS - 1, "turn")
            with sp.Fori(0, PAIRS - 1) as j:
                sync_step(sp, B - 1, j, "middle")
            sync_step(sp, B - 1, PAIRS - 1, "end")
            for n in range(2):
                sp.wait_ge(done_free[n], 16 * (B * PROJ_GROUPS // 2 + 1))

        def split_lo(pool, b):
            for c in range(CT):
                pool.wait_ge(xn_full_ready, b * CT + (c + 1))
                pool.tensor_tensor(xn[:, 1, c, :], tile_of(c), xn[:, 0, c, :].bitcast(F32), ALU.subtract)\
                    .then_inc(xn_ready, 1)

        @block.gpsimd
        def _(pool):
            with pool.Fori(0, B - 1) as b:
                split_lo(pool, b)
                pool.wait_ge(xn_ready, (b + 1) * CT)
                load_image(pool, b + 1, x_loaded)
            split_lo(pool, B - 1)

        def group_root(act, b, use):
            act.wait_ge(acc_free, use + 1)
            nc.scalar.activation(root[:], var_g[:], ACT.Sqrt).then_inc(root_ready, 1)

        def normalise(act, b, c):
            act.wait_ge(xn_hi_ready, b * CT + (c + 1))
            nc.scalar.activation(tile_of(c), tile_of(c), ACT.Identity,
                                 bias=shift_c[:, c:c + 1], scale=scale_c[:, c:c + 1]).then_inc(xn_full_ready, 1)

        def qk_hi(act, n, i, use, slot, heads=(0, 1)):
            which, tc = QK_GROUPS[i]
            if 0 in heads:
                act.wait_ge(acc_filled, use + 1)
            if i == 0:
                act.wait_ge(pair_bias_ready, n + 1)
            for h in heads:
                rows = slice(h * CH, (h + 1) * CH)
                for to in ((slice(0, CH), slice(CH, P)) if which else (rows,)):
                    stack = k_stack[to, h, 0, half(tc)] if which else q_stack[to, h, half(tc)]
                    last = nc.scalar.activation(stack, acc[rows, slot, :], ACT.Identity,
                                                bias=bias_pair[rows, which:which + 1])
                last.then_inc(qk_hi_ready, 1)

        def softmax_exp(act, g, i, first=False):
            act.wait_ge(max_ready, g * ITEMS + (i + 1))
            if not first:
                act.wait_ge(transposed, g * 2 * ITEMS + (2 * (i - 1) if i >= 2 else 0))
            nc.scalar.activation(probs[:, i % 2, :], scores[:, i % 2, :], ACT.Exp, bias=neg_max[:, i:i + 1],
                                 accum_out=row_sum[:, i:i + 1]).then_inc(exp_done, 1)

        def copy_turned(act, b, j, kind, i):
            g = b * PAIRS + j
            c, h, t = i // 4, i % 2, i // 2 % 2
            if i == 0:
                act.wait_ge(acc_filled, acc_base(b, j))
            elif i % 4 == 0 and c >= 2:
                act.wait_ge(acc_filled, acc_base(b, j) + (use_chunk(kind, c - 2) + 1))
            for k in range(2):
                act.wait_ge(transposed, g * 2 * ITEMS + (2 * i + k + 1))
                nc.scalar.activation(probs_t[:, c % 2, h, 4 * k:4 * k + 4, t * P:(t + 1) * P], turned[:, k, :, :],
                                     ACT.Copy).then_inc(probs_t_ready, 1)

        def split_attn_hi(act, b, all_out):
            act.wait_ge(acc_free, all_out)
            for c in range(PAIRS):
                nc.scalar.activation(attn_split[:, 0, c, :], attn[:, c * L:(c + 1) * L], ACT.Copy)\
                  .then_inc(attn_hi_ready, 1)

        def scalar_step(act, b, j, kind):
            g = b * PAIRS + j
            base = acc_base(b, j)
            last_qk_slots = (1, 2) if kind == "turn" else (3, 4)
            for i in range(ITEMS - 2):
                copy_turned(act, b, j, kind, i)
                softmax_exp(act, g, i + 2)
                if i in last_qk_slots:
                    qk_hi(act, g, 3, base + USE_LAST_QK, bank(USE_LAST_QK), (i - last_qk_slots[0],))
                if kind == "turn" and i == 4:
                    group_root(act, b + 1, base + (USE_AVERAGE + 1))
                if kind == "turn" and i in (6, 8, 10, 12):
                    normalise(act, b + 1, i // 2 - 3)
            for i in range(2):
                if kind != "end":
                    qk_hi(act, g + 1, i, base + use_qk(kind, i), bank(use_qk(kind, i)))
                copy_turned(act, b, j, kind, ITEMS - 2 + i)
            if kind != "end":
                qk_hi(act, g + 1, 2, base + use_qk(kind, 2), bank(use_qk(kind, 2)))
                softmax_exp(act, g + 1, 0)
                softmax_exp(act, g + 1, 1)
            if kind != "middle":
                split_attn_hi(act, b, base + (use_chunk(kind, CHUNKS - 1) + 1))

        @block.scalar
        def _(act):
            act.wait_ge(w_v_loaded, 16)
            nc.scalar.activation(w_v[:, 0, :, :], w_raw[:, :, 2 * C:3 * C], ACT.Copy).then_inc(w_hi_ready, 1)
            group_root(act, 0, 1)
            for c in range(CT):
                normalise(act, 0, c)
            act.wait_ge(w_qk_raw_loaded, 16)
            for which, scale in enumerate((QSCALE, 1.0)):
                nc.scalar.activation(split_parts[which][0], w_raw[:, :, which * C:(which + 1) * C], ACT.Copy,
                                     scale=scale).then_inc(w_hi_ready, 1)
            act.wait_ge(w_o_loaded, 16)
            nc.scalar.activation(w_o[:, 0, :, :], w_o_raw, ACT.Copy).then_inc(w_hi_ready, 1)
            act.wait_ge(w_stored, 16 * 4 * PAIRS)
            for i in range(3):
                qk_hi(act, 0, i, 2 + ST + i, i % 2)
            softmax_exp(act, 0, 0, first=True)
            softmax_exp(act, 0, 1, first=True)

            with act.Fori(0, B - 1) as b:
                with act.Fori(0, PAIRS - 1) as j:
                    scalar_step(act, b, j, "middle")
                scalar_step(act, b, PAIRS - 1, "turn")
            with act.Fori(0, PAIRS - 1) as j:
                scalar_step(act, B - 1, j, "middle")
            scalar_step(act, B - 1, PAIRS - 1, "end")

        def channel_stats(dve, c, h):
            return nc.vector.bn_stats(bn[:, bass.ds((c * 2 + h) * 6, 6)], x_img[:, bass.ds(c * L + h * HALF, HALF)])

        def split_lo_weights(dve, raw, hi, lo, scale, n):
            dve.wait_ge(w_hi_ready, n)
            nc.vector.scalar_tensor_tensor(lo, raw, scale, hi.bitcast(F32),
                                           ALU.mult, ALU.subtract).then_inc(w_lo_ready, 1)

        def sum_of_means(dve, b):
            dve.wait_ge(stat_link, b * STAT_LINKS + 1)
            nc.vector.tensor_reduce(sum_means[:], quarter(1).rearrange("p (c q) -> p c q", q=QUARTERS), AX.X, ALU.add)\
              .then_inc(stat_link, 1)

        def quarter(field):
            return bn[:].rearrange("p (q f) -> p q f", f=3)[:, :, field]

        def group_mean(dve, b, use, slot):
            base = b * STAT_LINKS
            dve.wait_ge(acc_filled, use + 1)
            nc.vector.tensor_scalar(mean_g[:], acc[:, slot, 0:CT], 1.0 / QUARTERS, None, ALU.mult).then_inc(acc_free, 1)
            dve.wait_ge(acc_free, use + 1)
            for c in range(CT):
                q = slice(c * QUARTERS, (c + 1) * QUARTERS)
                last = nc.vector.tensor_scalar(dist[:, q], quarter(1)[:, q], mean_g[:, c:c + 1], None, ALU.subtract)
            last.then_inc(stat_link, 1)
            dve.wait_ge(stat_link, base + 3)
            nc.vector.tensor_tensor(dist_sq[:], dist[:], dist[:], ALU.mult).then_inc(stat_link, 1)
            dve.wait_ge(stat_link, base + 4)
            nc.vector.scalar_tensor_tensor(dist[:], quarter(2), 1.0 * QUARTERS / L, dist_sq[:], ALU.mult, ALU.add)\
              .then_inc(stat_link, 1)
            dve.wait_ge(stat_link, base + 5)
            nc.vector.tensor_reduce(spread[:], dist[:].rearrange("p (c q) -> p c q", q=QUARTERS), AX.X, ALU.add)\
              .then_inc(stat_link, 1)

        def group_variance(dve, b, use, slot):
            dve.wait_ge(acc_filled, use + 1)
            nc.vector.tensor_scalar(var_g[:], acc[:, slot, 0:CT], 1.0 / QUARTERS, EPS, ALU.mult, ALU.add).then_inc(acc_free, 1)

        def group_affine(dve, b):
            base = b * STAT_LINKS
            dve.wait_ge(root_ready, b + 1)
            nc.vector.reciprocal(rstd[:], root[:]).then_inc(stat_link, 1)
            dve.wait_ge(stat_link, base + 7)
            nc.vector.tensor_tensor(newton[:], rstd[:], rstd[:], ALU.mult).then_inc(stat_link, 1)
            dve.wait_ge(stat_link, base + 8)
            nc.vector.scalar_tensor_tensor(newton[:], newton[:], -0.5, var_g[:], ALU.mult, ALU.mult)\
              .then_inc(stat_link, 1)
            dve.wait_ge(stat_link, base + 9)
            nc.vector.scalar_tensor_tensor(rstd[:], newton[:], 1.5, rstd[:], ALU.add, ALU.mult).then_inc(stat_link, 1)
            dve.wait_ge(stat_link, base + 10)
            nc.vector.tensor_tensor(scale_c[:], rstd[:], gamma[:], ALU.mult).then_inc(affine_step, 1)
            dve.wait_ge(affine_step, b * 2 + 1)
            nc.vector.tensor_tensor(newton[:], mean_g[:], scale_c[:], ALU.mult).then_inc(affine_step, 1)
            dve.wait_ge(affine_step, b * 2 + 2)
            nc.vector.tensor_tensor(shift_c[:], beta[:], newton[:], ALU.subtract).then_inc(affine_ready, 1)

        def normalise_hi(dve, b, c):
            dve.wait_ge(affine_ready, b + 1)
            nc.vector.tensor_scalar(xn[:, 0, c, :], tile_of(c), scale_c[:, c:c + 1], shift_c[:, c:c + 1],
                                    ALU.mult, ALU.add).then_inc(xn_hi_ready, 1)

        def v_out(dve, b, st, use, slot, first=False):
            dve.wait_ge(acc_filled, use + 1)
            if st == 0 and not first:
                dve.wait_ge(v_pair_loaded, b * PAIRS * 16)
            nc.vector.tensor_tensor(v_img[:, st, :], acc[:, slot, :], bias_v[:], ALU.add).then_inc(acc_free, 1)

        def pair_bias(dve, j):
            nc.vector.tensor_scalar(bias_pair[:].rearrange("p (k o) -> p k o", o=1), bias_qk[:, :, bass.ds(j, 1)], 1.0,
                                    None, ALU.mult).then_inc(pair_bias_ready, 1)

        def qk_lo(dve, n, i, slot, heads=(0, 1)):
            which, tc = QK_GROUPS[i]
            for h in heads:
                dve.wait_ge(qk_hi_ready, n * 8 + (2 * i + h + 1))
                rows, others = slice(h * CH, (h + 1) * CH), slice((1 - h) * CH, (2 - h) * CH)
                for to in ((slice(0, CH), slice(CH, P)) if which else (others,)):
                    stack = k_stack[to, h, 1, half(tc)] if which else q_stack[to, h, half(tc)]
                    hi = k_stack[rows, h, 0, half(tc)] if which else q_stack[rows, h, half(tc)]
                    last = nc.vector.scalar_tensor_tensor(stack, acc[rows, slot, :], bias_pair[rows, which:which + 1],
                                                          hi.bitcast(F32), ALU.add, ALU.subtract)
            if 1 in heads:
                last.then_inc(acc_free, 1)

        def row_max(dve, g, i):
            dve.wait_ge(scores_ready, g * ITEMS + (i + 1))
            nc.vector.tensor_reduce(neg_max[:, i:i + 1], scores[:, i % 2, :], AX.X, ALU.max, negate=True)\
              .then_inc(max_ready, 1)

        def divide(dve, g, i):
            dve.wait_ge(exp_done, g * ITEMS + (i + 1))
            nc.vector.reciprocal(row_inv[:, i:i + 1], row_sum[:, i:i + 1]).then_inc(inv_ready, 1)
            dve.wait_ge(inv_ready, g * ITEMS + (i + 1))
            nc.vector.tensor_scalar(probs[:, i % 2, :], probs[:, i % 2, :], row_inv[:, i:i + 1], None, ALU.mult)\
              .then_inc(probs_ready, 1)

        def attn_out(dve, j, c, base, use):
            dve.wait_ge(acc_filled, base + (use + 1))
            nc.vector.tensor_copy(attn[:, bass.ds(j * L + c * CQ, CQ)], acc[:, bank(use), 0:CQ]).then_inc(acc_free, 1)

        def split_attn_lo(dve, b, c):
            dve.wait_ge(attn_hi_ready, b * PAIRS + (c + 1))
            nc.vector.tensor_tensor(attn_split[:, 1, c, :], attn[:, c * L:(c + 1) * L],
                                    attn_split[:, 0, c, :].bitcast(F32), ALU.subtract).then_inc(attn_lo_ready, 1)

        def proj_out(dve, b, n, base, use):
            ot = n // TC
            dve.wait_ge(acc_filled, base + (use + 1))
            dve.wait_ge(resid_loaded[n % 2], (b * (PROJ_GROUPS // 2) + (n // 2 + 1)) * 16)
            dve.wait_ge(done_free[n % 2], (b * (PROJ_GROUPS // 2) + (n // 2 + 1)) * 16)
            nc.vector.scalar_tensor_tensor(done[:, n % 2, :], acc[:, bank(use), :], bias_o[:, ot:ot + 1],
                                           resid[:, n % 2, :], ALU.add, ALU.add).then_inc(acc_free, 1)

        def vector_step(dve, b, j, kind, stats=True):
            g = b * PAIRS + j
            base = acc_base(b, j)
            if stats:
                dve.wait_ge(x_loaded, (b + 1) * 16)
            last_qk_slots = (2, 3) if kind == "turn" else (4, 5)
            for i in range(ITEMS - 2):
                row_max(dve, g, i + 2)
                if i == last_qk_slots[1]:
                    qk_lo(dve, g, 3, bank(USE_LAST_QK), (1,))
                divide(dve, g, i + 1)
                if i == last_qk_slots[0]:
                    qk_lo(dve, g, 3, bank(USE_LAST_QK), (0,))
                if i == ITEMS // 2 and kind != "end":
                    pair_bias(dve, j + 1 if kind == "middle" else 0)
                if i in (8, 12):
                    attn_out(dve, j, i // 4 - 2, base, use_chunk(kind, i // 4 - 2))
                if stats and i < 2:
                    last = channel_stats(dve, j, i)
                if kind == "turn":
                    if i == 1:
                        last.then_inc(stat_link, 1)
                        sum_of_means(dve, b + 1)
                    elif i == 3:
                        group_mean(dve, b + 1, base + USE_AVERAGE, bank(USE_AVERAGE))
                    elif i == 4:
                        group_variance(dve, b + 1, base + (USE_AVERAGE + 1), bank(USE_AVERAGE + 1))
                    elif i == 5:
                        group_affine(dve, b + 1)
                        dve.wait_ge(acc_filled, base + (USE_LAST_QK + 1))
                        normalise_hi(dve, b + 1, 0)
                    elif i in (7, 9, 11):
                        normalise_hi(dve, b + 1, (i - 5) // 2)
            divide(dve, g, ITEMS - 1)
            attn_out(dve, j, 2, base, use_chunk(kind, 2))
            if kind != "end":
                dve.wait_ge(pair_bias_ready, g + 2)
                for i in range(3):
                    qk_lo(dve, g + 1, i, bank(use_qk(kind, i)))
                row_max(dve, g + 1, 0)
                row_max(dve, g + 1, 1)
                divide(dve, g + 1, 0)
            attn_out(dve, j, CHUNKS - 1, base, use_chunk(kind, CHUNKS - 1))
            if kind == "turn":
                for st in range(ST):
                    v_out(dve, b + 1, st, base + use_v(st), bank(use_v(st)))
                    if st < PAIRS:
                        split_attn_lo(dve, b, st)
            elif kind == "end":
                for c in range(PAIRS):
                    split_attn_lo(dve, b, c)
            if kind != "middle":
                for n in range(PROJ_GROUPS):
                    proj_out(dve, b, n, base, use_out(kind, n))

        @block.vector
        def _(dve):
            dve.wait_ge(first_x_loaded, 16)
            for n in range(2 * CT):
                last = channel_stats(dve, n // 2, n % 2)
            last.then_inc(stat_link, 1)
            sum_of_means(dve, 0)
            group_mean(dve, 0, 0, 0)
            group_variance(dve, 0, 1, 1)
            split_lo_weights(dve, w_raw[:, :, 2 * C:3 * C], w_v[:, 0, :, :], w_v[:, 1, :, :], 1.0, 1)
            dve.wait_ge(group_loaded, 48)
            group_affine(dve, 0)
            for c in range(CT):
                normalise_hi(dve, 0, c)
            for which, scale in enumerate((QSCALE, 1.0)):
                split_lo_weights(dve, w_raw[:, :, which * C:(which + 1) * C], *split_parts[which], scale, 2 + which)
            split_lo_weights(dve, w_o_raw, w_o[:, 0, :, :], w_o[:, 1, :, :], 1.0, 4)
            dve.wait_ge(consts_loaded, 16 * 4)
            nc.vector.tensor_scalar(bias_qk[:, 0, :], bias_qkv[:, 0:CT], QSCALE, None, ALU.mult).then_inc(bias_ready, 1)
            nc.vector.tensor_copy(bias_qk[:, 1, :], bias_qkv[:, CT:2 * CT]).then_inc(bias_ready, 1)
            dve.wait_ge(bias_ready, 2)
            pair_bias(dve, 0)
            for st in range(ST):
                v_out(dve, 0, st, 2 + st, st % 2, first=True)
            dve.wait_ge(pair_bias_ready, 1)
            for i in range(3):
                qk_lo(dve, 0, i, i % 2)
            row_max(dve, 0, 0)
            row_max(dve, 0, 1)
            divide(dve, 0, 0)

            with dve.Fori(0, B - 1) as b:
                with dve.Fori(0, PAIRS - 1) as j:
                    vector_step(dve, b, j, "middle")
                vector_step(dve, b, PAIRS - 1, "turn")
            with dve.Fori(0, PAIRS - 1) as j:
                vector_step(dve, B - 1, j, "middle", stats=False)
            vector_step(dve, B - 1, PAIRS - 1, "end", stats=False)

        def bank_free(pe, use, first=False):
            if not first:
                pe.wait_ge(acc_free, use - 1)

        def group_average(pe, b, which, use, slot, first=False):
            pe.wait_ge(stat_link, b * STAT_LINKS + (2, 6)[which])
            bank_free(pe, use, first)
            src = (sum_means, spread)[which][:]
            nc.tensor.matmul(acc[:, slot, 0:CT], group[:], src, start=True, stop=True).then_inc(acc_filled, 1)

        def split_product(terms, out_ap, part=slice(None)):
            for n in range(len(terms))[part]:
                last = nc.tensor.matmul(out_ap, *terms[n], start=n == 0, stop=n == len(terms) - 1)
            return last

        def project_v(pe, st, use, slot):
            px = slice(st * P, (st + 1) * P)
            bank_free(pe, use)
            split_product([(xn[:, a, c, px], w_v[:, w, c, :]) for c in range(CT) for a, w in ((0, 0), (0, 1), (1, 0))],
                          acc[:, slot, :]).then_inc(acc_filled, 1)

        def project_qk(pe, i, use, slot, part=0, parts=1):
            which, tc = QK_GROUPS[i]
            if part == 0:
                bank_free(pe, use)
            terms = [(w_qk[:, w, c, which, :], xn[:, a, c, half(tc)])
                     for c in range(CT) for w, a in ((0, 0), (0, 1), (1, 0))]
            n = len(terms) // parts
            last = split_product(terms, acc[:, slot, :], slice(part * n, (part + 1) * n))
            if part == parts - 1:
                last.then_inc(acc_filled, 1)

        def score(pe, g, i, written=None, first=False):
            t, h = divmod(i, 2)
            if written is not None:
                pe.wait_ge(acc_free, written)
            if not first:
                pe.wait_ge(exp_done, g * ITEMS + (i - 1))
            lhs = q_stack[:, h, t * P:(t + 1) * P]
            for tc in range(TC):
                nc.tensor.matmul(scores[:, i % 2, half(tc)], lhs, k_stack[:, h, 0, half(tc)], start=True, stop=False)
                last = nc.tensor.matmul(scores[:, i % 2, half(tc)], lhs, k_stack[:, h, 1, half(tc)],
                                        start=False, stop=True)
            last.then_inc(scores_ready, 1)

        def transpose(pe, g, i):
            pe.wait_ge(probs_ready, g * ITEMS + (i + 1))
            for k in range(2):
                if i:
                    pe.wait_ge(probs_t_ready, g * 2 * ITEMS + (2 * i - 1 + k))
                for n in range(4):
                    s = (4 * k + n) * P
                    last = nc.tensor.transpose(turned[:, k, n, :], probs[:, i % 2, s:s + P], ident[:])
                last.then_inc(transposed, 1)

        def attend(pe, g, c, quarters, use, slot):
            if 0 in quarters:
                pe.wait_ge(probs_t_ready, g * 2 * ITEMS + 8 * (c + 1))
                if c == 0:
                    pe.wait_ge(v_pair_loaded, (g + 1) * 16)
                bank_free(pe, use)
            for st in range(quarters[0] * ST // 4, (quarters[-1] + 1) * ST // 4):
                for h in range(2):
                    rows = slice(h * CH, (h + 1) * CH)
                    last = nc.tensor.matmul(acc[rows, slot, 0:CQ], v_pair[:, st, rows], probs_t[:, c % 2, h, st, :],
                                            start=st == 0, stop=st == ST - 1)
            if 3 in quarters:
                last.then_inc(acc_filled, 1)

        def project_out(pe, b, n, use, slot):
            ot, tc = divmod(n, TC)
            bank_free(pe, use)
            if n == 0:
                pe.wait_ge(attn_lo_ready, (b + 1) * PAIRS)
            split_product([(w_o[:, w, c, ot * P:(ot + 1) * P], attn_split[:, a, c, half(tc)])
                           for c in range(CT) for w, a in ((0, 0), (0, 1), (1, 0))],
                          acc[:, slot, :]).then_inc(acc_filled, 1)

        def tensor_step(pe, b, j, kind):
            g = b * PAIRS + j
            base = acc_base(b, j)
            spread_chunks = {4 * c + 4 + q: (c, [q]) for c in range(2) for q in range(4)}
            spread_chunks.update({12: (2, [0, 1]), 13: (2, [2, 3])})
            for i in range(ITEMS - 2):
                score(pe, g, i + 2, base + (USE_LAST_QK + 1) if i + 2 == ITEMS // 2 else None)
                parts = 2 if kind == "turn" else 4
                if i < parts:
                    project_qk(pe, 3, base + USE_LAST_QK, bank(USE_LAST_QK), i, parts)
                transpose(pe, g, i)
                if i in spread_chunks:
                    c, quarters = spread_chunks[i]
                    attend(pe, g, c, quarters, base + use_chunk(kind, c), bank(use_chunk(kind, c)))
                if kind == "turn" and i in (3, 4):
                    use = USE_AVERAGE + i - 3
                    group_average(pe, b + 1, i - 3, base + use, bank(use))
            last_chunk = use_chunk(kind, CHUNKS - 1)
            if kind == "end":
                transpose(pe, g, ITEMS - 2)
                transpose(pe, g, ITEMS - 1)
                attend(pe, g, CHUNKS - 1, [0, 1, 2, 3], base + last_chunk, bank(last_chunk))
            else:
                pe.wait_ge(w_qk_loaded, (g + 2) * 16)
                if kind == "turn":
                    pe.wait_ge(xn_ready, (b + 2) * CT)
                for i in range(3):
                    project_qk(pe, i, base + use_qk(kind, i), bank(use_qk(kind, i)))
                    if i < 2:
                        transpose(pe, g, ITEMS - 2 + i)
                attend(pe, g, CHUNKS - 1, [0, 1], base + last_chunk, bank(last_chunk))
                score(pe, g + 1, 0, base + (use_qk(kind, 2) + 1))
                score(pe, g + 1, 1)
                attend(pe, g, CHUNKS - 1, [2, 3], base + last_chunk, bank(last_chunk))
            if kind == "turn":
                for st in range(ST):
                    project_v(pe, st, base + use_v(st), bank(use_v(st)))
            if kind != "middle":
                for n in range(PROJ_GROUPS):
                    use = use_out(kind, n)
                    project_out(pe, b, n, base + use, bank(use))

        @block.tensor
        def _(pe):
            pe.wait_ge(group_loaded, 48)
            group_average(pe, 0, 0, 0, 0, first=True)
            group_average(pe, 0, 1, 1, 1, first=True)
            pe.wait_ge(w_lo_ready, 1)
            pe.wait_ge(xn_ready, CT)
            for st in range(ST):
                project_v(pe, st, 2 + st, st % 2)
            pe.wait_ge(w_qk_loaded, 16)
            pe.wait_ge(consts_loaded, 16 * 4)
            for i in range(3):
                project_qk(pe, i, 2 + ST + i, i % 2)
            score(pe, 0, 0, ACC_PROLOGUE, first=True)
            score(pe, 0, 1, first=True)

            with pe.Fori(0, B - 1) as b:
                with pe.Fori(0, PAIRS - 1) as j:
                    tensor_step(pe, b, j, "middle")
                tensor_step(pe, b, PAIRS - 1, "turn")
            with pe.Fori(0, PAIRS - 1) as j:
                tensor_step(pe, B - 1, j, "middle")
            tensor_step(pe, B - 1, PAIRS - 1, "end")

    return nc


def kernel(x, L0_conv_gn_w, L0_conv_gn_b, L0_conv_qkv_w, L0_conv_qkv_b, L0_conv_proj_w, L0_conv_proj_b):
    import numpy as np
    import concourse.bacc as bacc
    from concourse.bass_utils import run_bass_kernel_spmd

    def columns(a):
        return np.ascontiguousarray(np.asarray(a).reshape(-1, P).T)

    same_group = np.arange(P)[:, None] // (C // GROUPS) == np.arange(P)[None, :] // (C // GROUPS)
    arrays = {
        "x": np.ascontiguousarray(np.asarray(x).reshape(B, C, L)),
        "w_qkv_t": np.ascontiguousarray(np.asarray(L0_conv_qkv_w).T),
        "w_proj_t": np.ascontiguousarray(np.asarray(L0_conv_proj_w).T),
        "b_qkv": columns(L0_conv_qkv_b),
        "b_v_row": np.ascontiguousarray(np.broadcast_to(np.asarray(L0_conv_qkv_b)[None, 2 * C:], (P, C))),
        "b_proj": columns(L0_conv_proj_b),
        "gn_w": columns(L0_conv_gn_w),
        "gn_b": columns(L0_conv_gn_b),
        "identity": np.eye(P, dtype=np.float32),
        "group_mean": same_group.astype(np.float32) / np.float32(C // GROUPS),
    }
    nc = bacc.Bacc("TRN2", target_bir_lowering=False, num_devices=1)
    args = [nc.dram_tensor(n, a.shape, F32, kind="ExternalInput").ap() for n, a in arrays.items()]
    out = nc.dram_tensor("out", (B, C, L), F32, kind="ExternalOutput").ap()
    build(nc, *args, out)
    result = run_bass_kernel_spmd(nc, [arrays], core_ids=[0])
    return result.results[0]["out"].reshape(B, C, 32, 32)
```

```python
from contextlib import ExitStack

import concourse.bass as bass
import concourse.mybir as mybir

F32 = mybir.dt.float32
F32R = mybir.dt.float32r
ALU = mybir.AluOpType
ACT = mybir.ActivationFunctionType
AX = mybir.AxisListType

P = 128
B, C, L = 16, 512, 1024
HEADS, GROUPS = 8, 32
CH = C // HEADS
CT = C // P
PAIRS = HEADS // 2
ST = L // P
HALF = 512
TC = L // HALF
ITEMS = 2 * ST
CHUNKS = ITEMS // 4
CQ = L // CHUNKS
EPS = 1e-5
QUARTERS = 4
QSCALE = 1.0 / CH ** 0.5

ACC_PROLOGUE = ST + 3
ACC_STEP = CHUNKS + 2 * TC
PROJ_GROUPS = CT * TC
ACC_TURN = ST + PROJ_GROUPS
SPLIT_SLOTS = (5, 7, 9, 11)
TURNS = ("turn", "last turn")
STAT_LINKS = 9


def build(nc, x, w_qkv_t, w_proj_t, b_qkv, b_v_row, b_proj, gn_w, gn_b, ident_in, group_in, out):
    ctx = ExitStack()
    with ctx:
        def sb(name, shape, dt=F32):
            return ctx.enter_context(nc.sbuf_tensor(name, shape, dt))

        def ps(name, shape):
            return ctx.enter_context(nc.psum_tensor(name, shape, F32))

        def sem(name):
            return ctx.enter_context(nc.semaphore(name))

        w_v = sb("w_v", [P, 2, CT, C], F32R)
        w_o = sb("w_o", [P, 2, CT, C], F32R)
        w_qk = sb("w_qk", [P, 2, CT, 2, P], F32R)
        x_img = sb("x_img", [P, CT * L])
        xn = sb("xn", [P, 2, CT, L], F32R)
        q_stack = sb("q_stack", [P, 2, L], F32R)
        q_other = sb("q_other", [P, L], F32R)
        k_stack = sb("k_stack", [P, 2, L], F32R)
        k_lo = sb("k_lo", [P, 2, HALF], F32R)
        v_img = sb("v_img", [P, ST, C])
        v_pair = sb("v_pair", [P, ST, P])
        probs = sb("probs", [P, 2, L])
        with nc.sbuf_tensor("attn_split", [P, 2, PAIRS, L], F32R) as attn_split:
            pass
        probs_t = sb("probs_t", [P, 2, 2, ST, CQ])
        with nc.sbuf_tensor("w_spare", [P, CT, C], F32R) as w_spare:
            pass
        attn = sb("attn", [P, PAIRS * L])
        resid = sb("resid", [P, 2, HALF])
        done = sb("done", [P, 2, HALF])
        bias_qkv = sb("bias_qkv", [P, 3 * CT])
        bias_qk = sb("bias_qk", [P, 2, PAIRS])
        bias_pair = sb("bias_pair", [P, 2])
        bias_v = sb("bias_v", [P, C])
        bias_o = sb("bias_o", [P, CT])
        gamma = sb("gamma", [P, CT])
        beta = sb("beta", [P, CT])
        ident = sb("ident", [P, P])
        group = sb("group", [P, P])
        neg_max = sb("neg_max", [P, ITEMS])
        row_sum = sb("row_sum", [P, ITEMS])
        row_inv = sb("row_inv", [P, ITEMS])
        bn = sb("bn", [P, CT * 2 * 6])
        sum_means = sb("sum_means", [P, CT])
        dist = sb("dist", [P, CT * QUARTERS])
        dist_sq = sb("dist_sq", [P, CT * QUARTERS])
        mean_g = sb("mean_g", [P, CT])
        spread = sb("spread", [P, CT])
        var_g = sb("var_g", [P, CT])
        root = sb("root", [P, CT])
        rstd = sb("rstd", [P, CT])
        newton = sb("newton", [P, CT])
        scale_c = sb("scale_c", [P, CT])
        shift_c = sb("shift_c", [P, CT])

        scores = ps("scores", [P, 2, L])
        turned = ps("turned", [P, 2, 4, P])
        acc = ps("acc", [P, 2, HALF])

        w_qk_dram = nc.dram_tensor("w_qk_dram", [PAIRS, P, 2, CT, 2, P], F32R, kind="Internal").ap()

        consts_loaded = sem("consts_loaded")
        group_loaded = sem("group_loaded")
        w_v_loaded = sem("w_v_loaded")
        w_qk_raw_loaded = sem("w_qk_raw_loaded")
        w_o_loaded = sem("w_o_loaded")
        w_hi_ready = sem("w_hi_ready")
        w_lo_ready = sem("w_lo_ready")
        w_stored = sem("w_stored")
        bias_ready = sem("bias_ready")
        pair_bias_ready = sem("pair_bias_ready")
        w_qk_loaded = sem("w_qk_loaded")
        first_x_loaded = [sem(f"first_x_loaded_{c}") for c in range(CT)]
        x_loaded = sem("x_loaded")
        bn_ready = sem("bn_ready")
        stat_link = sem("stat_link")
        root_ready = sem("root_ready")
        affine_step = sem("affine_step")
        affine_ready = sem("affine_ready")
        xn_hi_ready = sem("xn_hi_ready")
        xn_full_ready = sem("xn_full_ready")
        xn_ready = sem("xn_ready")
        averaged = sem("averaged")
        average_taken = sem("average_taken")
        acc_filled = sem("acc_filled")
        acc_free = sem("acc_free")
        qk_hi_ready = sem("qk_hi_ready")
        q_piece_ready = sem("q_piece_ready")
        q_other_ready = sem("q_other_ready")
        v_pair_loaded = sem("v_pair_loaded")
        scores_ready = sem("scores_ready")
        max_ready = sem("max_ready")
        exp_done = sem("exp_done")
        inv_ready = sem("inv_ready")
        probs_ready = sem("probs_ready")
        transposed = sem("transposed")
        probs_t_ready = sem("probs_t_ready")
        attn_hi_ready = sem("attn_hi_ready")
        attn_lo_ready = sem("attn_lo_ready")
        resid_loaded = [sem(f"resid_loaded_{n}") for n in range(2)]
        done_free = [sem(f"done_free_{n}") for n in range(2)]

        QK_GROUPS = [(1, 0), (1, 1), (0, 0), (0, 1)]

        def acc_base(b, j):
            return (b * PAIRS + j) * ACC_STEP + b * ACC_TURN + ACC_PROLOGUE

        def bank(use):
            return (ACC_PROLOGUE + use) % 2

        USE_LAST_QK = 0
        average = [turned[:, 0, 0, k * CT:(k + 1) * CT] for k in range(2)]

        def use_chunk(kind, c):
            return 1 + c + (3 if kind != "end" and c == CHUNKS - 1 else 0)

        def use_qk(kind, i):
            return use_chunk(kind, CHUNKS - 2) + 1 + i

        def use_v(st):
            return ACC_STEP + st

        def use_out(kind, n):
            return (1 + CHUNKS if kind == "end" else ACC_STEP + ST) + n

        def half(tc):
            return slice(tc * HALF, (tc + 1) * HALF)

        def pieces_of(which, tc):
            if which:
                return [[(h, slice(0, HALF), half(tc))] for h in range(2)]
            return [[(h, slice(k * CQ, (k + 1) * CQ), slice(tc * HALF + k * CQ, tc * HALF + (k + 1) * CQ))
                     for h in range(2)] for k in range(2)]

        PIECES = [pieces_of(which, tc) for which, tc in QK_GROUPS]
        HI_PARTS = sum(len(piece) for pieces in PIECES for piece in pieces)

        def tile_of(c):
            return x_img[:, c * L:(c + 1) * L]

        probs_t_flat = probs_t[:].rearrange("p a h s q -> p (a h s q)")
        w_raw = probs_t_flat[:, 0:CT * 3 * C].rearrange("p (c o) -> p c o", c=CT)
        w_o_raw = probs_t_flat[:, CT * 3 * C:CT * 4 * C].rearrange("p (c o) -> p c o", c=CT)
        def as_weights(tile):
            return tile.rearrange("p h l -> p (h l)").rearrange("p (c o) -> p c o", c=CT)

        split_parts = ((as_weights(k_stack[:]), w_spare[:]),
                       (as_weights(q_stack[:]),
                        w_qk[:].rearrange("p s c g o -> p (s c g o)").rearrange("p (c o) -> p c o", c=CT)))

        block = ctx.enter_context(nc.Block())

        def load_image(pool, b):
            pool.dma_start(x_img[:].rearrange("p (c l) -> p c l", c=CT),
                           x[b].rearrange("(c p) l -> p c l", p=P)).then_inc(x_loaded, 16)

        def load_w_qk(sp, j):
            sp.dma_start(w_qk[:].bitcast(F32).rearrange("p s c g o -> p (s c g o)"),
                         w_qk_dram[j].bitcast(F32).rearrange("p s c g o -> p (s c g o)")).then_inc(w_qk_loaded, 16)

        def sync_step(sp, b, j, kind):
            g = b * PAIRS + j
            base = acc_base(b, j)
            sp.wait_ge(acc_free, base)
            sp.dma_start(v_pair[:], v_img[:, :, bass.ds(j * P, P)]).then_inc(v_pair_loaded, 16)
            if kind != "end":
                sp.wait_ge(acc_free, base + (USE_LAST_QK + 1))
                load_w_qk(sp, j + 1 if kind == "middle" else 0)
            if kind == "middle":
                return
            for n in range(PROJ_GROUPS + 1):
                if n < PROJ_GROUPS:
                    if n >= 2:
                        sp.wait_ge(acc_free, base + (use_out(kind, n - 2) + 1))
                    ot, tc = divmod(n, TC)
                    sp.dma_start(resid[:, n % 2, :], x[b, ot * P:(ot + 1) * P, half(tc)])\
                      .then_inc(resid_loaded[n % 2], 16)
                if n:
                    sp.wait_ge(acc_free, base + (use_out(kind, n - 1) + 1))
                    ot, tc = divmod(n - 1, TC)
                    sp.dma_start(out[b, ot * P:(ot + 1) * P, half(tc)], done[:, (n - 1) % 2, :])\
                      .then_inc(done_free[(n - 1) % 2], 16)
        @block.sync
        def _(sp):
            for n in range(2):
                sp.sem_inc(done_free[n], 16)
            for dst, src in ((group, group_in), (gamma, gn_w), (beta, gn_b)):
                sp.dma_start(dst[:], src).then_inc(group_loaded, 16)
            for c in range(CT):
                sp.dma_start(tile_of(c), x[0, c * P:(c + 1) * P, :]).then_inc(first_x_loaded[c], 16)
            w_rows = w_qkv_t.rearrange("(c p) o -> p c o", p=P)
            sp.dma_start(w_raw[:, :, 2 * C:3 * C], w_rows[:, :, 2 * C:3 * C]).then_inc(w_v_loaded, 16)
            sp.dma_start(w_raw[:, :, 0:2 * C], w_rows[:, :, 0:2 * C]).then_inc(w_qk_raw_loaded, 16)
            for dst, src in ((bias_qkv, b_qkv), (bias_v, b_v_row), (bias_o, b_proj), (ident, ident_in)):
                sp.dma_start(dst[:], src).then_inc(consts_loaded, 16)
            sp.dma_start(w_o_raw, w_proj_t.rearrange("(c p) o -> p c o", p=P)).then_inc(w_o_loaded, 16)
            sp.wait_ge(w_lo_ready, 3)
            for which in range(2):
                for part in range(2):
                    for j in range(PAIRS):
                        sp.dma_start(w_qk_dram[j, :, part, :, which, :].bitcast(F32),
                                     split_parts[which][part].bitcast(F32)[:, :, j * P:(j + 1) * P])\
                          .then_inc(w_stored, 16)
            sp.wait_ge(w_stored, 16 * 4 * PAIRS)
            load_w_qk(sp, 0)

            with sp.Fori(0, B - 2) as b:
                with sp.Fori(0, PAIRS - 1) as j:
                    sync_step(sp, b, j, "middle")
                sync_step(sp, b, PAIRS - 1, "turn")
            for b, kind in ((B - 2, "last turn"), (B - 1, "end")):
                with sp.Fori(0, PAIRS - 1) as j:
                    sync_step(sp, b, j, "middle")
                sync_step(sp, b, PAIRS - 1, kind)
            for n in range(2):
                sp.wait_ge(done_free[n], 16 * (B * PROJ_GROUPS // 2 + 1))

        def split_lo(pool, b, tiles=range(CT)):
            for c in tiles:
                pool.wait_ge(xn_hi_ready, b * CT + (c + 1))
                pool.tensor_tensor(xn[:, 1, c, :], tile_of(c), xn[:, 0, c, :].bitcast(F32), ALU.subtract)\
                    .then_inc(xn_ready, 1)

        @block.gpsimd
        def _(pool):
            split_lo(pool, 0, range(0, CT // 2))
            pool.wait_ge(xn_ready, CT)
            load_image(pool, 1)
            pool.wait_ge(affine_ready, 2)
            for c in range(CT):
                pool.tensor_scalar(tile_of(c), tile_of(c), scale_c[:, c:c + 1], shift_c[:, c:c + 1], ALU.mult, ALU.add)\
                    .then_inc(xn_full_ready, 1)
            with pool.Fori(1, B - 1) as b:
                split_lo(pool, b)
                pool.wait_ge(xn_ready, (b + 1) * CT)
                load_image(pool, b + 1)
            split_lo(pool, B - 1)

        def group_root(act, b):
            act.wait_ge(average_taken, 2 * b + 2)
            nc.scalar.activation(root[:], var_g[:], ACT.Sqrt).then_inc(root_ready, 1)

        def normalise(act, b, c):
            act.wait_ge(affine_ready, b + 1)
            nc.scalar.activation(tile_of(c), tile_of(c), ACT.Identity,
                                 bias=shift_c[:, c:c + 1], scale=scale_c[:, c:c + 1]).then_inc(xn_full_ready, 1)

        def prepare(act, b):
            group_root(act, b)
            for c in range(CT):
                normalise(act, b, c)

        def qk_hi(act, n, i, use, slot, pieces=(0, 1)):
            if 0 in pieces:
                act.wait_ge(acc_filled, use + 1)
            if i == 0:
                act.wait_ge(pair_bias_ready, n + 1)
            which = QK_GROUPS[i][0]
            for k in pieces:
                if i >= 2 and k == 1:
                    act.wait_ge(q_piece_ready, n * 2 + (i - 1))
                for h, part, px in PIECES[i][k]:
                    rows = slice(h * CH, (h + 1) * CH)
                    nc.scalar.activation((k_stack if which else q_stack)[rows, h, px], acc[rows, slot, part],
                                         ACT.Identity, bias=bias_pair[rows, which:which + 1]).then_inc(qk_hi_ready, 1)

        def k_hi_twice(act, n, i):
            act.wait_ge(qk_hi_ready, n * HI_PARTS + (2 * i + 2))
            for h in range(2):
                rows, others = slice(h * CH, (h + 1) * CH), slice((1 - h) * CH, (2 - h) * CH)
                nc.scalar.activation(k_stack[others, h, half(i)], k_stack[rows, h, half(i)].bitcast(F32), ACT.Copy)

        def softmax_exp(act, g, i, first=False):
            act.wait_ge(max_ready, g * ITEMS + (i + 1))
            if not first:
                act.wait_ge(transposed, g * 2 * ITEMS + (2 * (i - 1) if i >= 2 else 0))
            nc.scalar.activation(probs[:, i % 2, :], scores[:, i % 2, :], ACT.Exp, bias=neg_max[:, i:i + 1],
                                 accum_out=row_sum[:, i:i + 1]).then_inc(exp_done, 1)

        def copy_turned(act, b, j, kind, i):
            g = b * PAIRS + j
            c, h, t = i // 4, i % 2, i // 2 % 2
            if i == 0:
                act.wait_ge(acc_filled, acc_base(b, j))
            elif i % 4 == 0 and c >= 2:
                act.wait_ge(acc_filled, acc_base(b, j) + (use_chunk(kind, c - 2) + 1))
            for k in range(2):
                act.wait_ge(transposed, g * 2 * ITEMS + (2 * i + k + 1))
                nc.scalar.activation(probs_t[:, c % 2, h, 4 * k:4 * k + 4, t * P:(t + 1) * P], turned[:, k, :, :],
                                     ACT.Copy).then_inc(probs_t_ready, 1)

        def split_attn_hi(act, b, all_out):
            act.wait_ge(acc_free, all_out)
            for c in range(PAIRS):
                nc.scalar.activation(attn_split[:, 0, c, :], attn[:, c * L:(c + 1) * L], ACT.Copy)\
                  .then_inc(attn_hi_ready, 1)

        def scalar_step(act, b, j, kind):
            g = b * PAIRS + j
            base = acc_base(b, j)
            for i in range(ITEMS - 2):
                copy_turned(act, b, j, kind, i)
                softmax_exp(act, g, i + 2)
                if i in (3, 5):
                    qk_hi(act, g, 3, base + USE_LAST_QK, bank(USE_LAST_QK), (i // 4,))
            for i in range(2):
                if kind != "end":
                    qk_hi(act, g + 1, i, base + use_qk(kind, i), bank(use_qk(kind, i)))
                copy_turned(act, b, j, kind, ITEMS - 2 + i)
                if kind != "end":
                    k_hi_twice(act, g + 1, i)
            if kind != "end":
                qk_hi(act, g + 1, 2, base + use_qk(kind, 2), bank(use_qk(kind, 2)))
                softmax_exp(act, g + 1, 0)
                softmax_exp(act, g + 1, 1)
            if kind != "middle":
                split_attn_hi(act, b, base + (use_chunk(kind, CHUNKS - 1) + 1))
            if kind == "turn":
                prepare(act, b + 2)

        @block.scalar
        def _(act):
            act.wait_ge(w_v_loaded, 16)
            nc.scalar.activation(w_v[:, 0, :, :], w_raw[:, :, 2 * C:3 * C], ACT.Copy).then_inc(w_hi_ready, 1)
            prepare(act, 0)
            act.wait_ge(w_qk_raw_loaded, 16)
            for which, scale in enumerate((QSCALE, 1.0)):
                nc.scalar.activation(split_parts[which][0], w_raw[:, :, which * C:(which + 1) * C], ACT.Copy,
                                     scale=scale).then_inc(w_hi_ready, 1)
            act.wait_ge(w_o_loaded, 16)
            nc.scalar.activation(w_o[:, 0, :, :], w_o_raw, ACT.Copy).then_inc(w_hi_ready, 1)
            act.wait_ge(w_stored, 16 * 4 * PAIRS)
            for i in range(3):
                qk_hi(act, 0, i, ST + i, i % 2)
                if i < TC:
                    k_hi_twice(act, 0, i)
                if i == 1:
                    group_root(act, 1)
            softmax_exp(act, 0, 0, first=True)
            softmax_exp(act, 0, 1, first=True)

            with act.Fori(0, B - 2) as b:
                with act.Fori(0, PAIRS - 1) as j:
                    scalar_step(act, b, j, "middle")
                scalar_step(act, b, PAIRS - 1, "turn")
            for b, kind in ((B - 2, "last turn"), (B - 1, "end")):
                with act.Fori(0, PAIRS - 1) as j:
                    scalar_step(act, b, j, "middle")
                scalar_step(act, b, PAIRS - 1, kind)

        def channel_stats(dve, n):
            last = nc.vector.bn_stats(bn[:, n * 6:(n + 1) * 6], x_img[:, n * HALF:(n + 1) * HALF])
            if n == 2 * CT - 1:
                last.then_inc(bn_ready, 1)

        def image_stats(dve, b, c):
            if c == 0:
                dve.wait_ge(x_loaded, b * 16)
            for h in range(2):
                channel_stats(dve, 2 * c + h)

        def split_lo_weights(dve, raw, hi, lo, scale, n):
            dve.wait_ge(w_hi_ready, n)
            nc.vector.scalar_tensor_tensor(lo, raw, scale, hi.bitcast(F32),
                                           ALU.mult, ALU.subtract).then_inc(w_lo_ready, 1)

        def sum_of_means(dve, b):
            dve.wait_ge(bn_ready, b + 1)
            nc.vector.tensor_reduce(sum_means[:], quarter(1).rearrange("p (c q) -> p c q", q=QUARTERS), AX.X, ALU.add)\
              .then_inc(stat_link, 1)

        def quarter(field):
            return bn[:].rearrange("p (q f) -> p q f", f=3)[:, :, field]

        def group_mean(dve, b):
            base = b * STAT_LINKS
            dve.wait_ge(averaged, 2 * b + 1)
            nc.vector.tensor_scalar(mean_g[:], average[0], 1.0 / QUARTERS, None, ALU.mult)\
              .then_inc(average_taken, 1)
            dve.wait_ge(average_taken, 2 * b + 1)
            for c in range(CT):
                q = slice(c * QUARTERS, (c + 1) * QUARTERS)
                last = nc.vector.tensor_scalar(dist[:, q], quarter(1)[:, q], mean_g[:, c:c + 1], None, ALU.subtract)
            last.then_inc(stat_link, 1)
            dve.wait_ge(stat_link, base + 2)
            nc.vector.tensor_tensor(dist_sq[:], dist[:], dist[:], ALU.mult).then_inc(stat_link, 1)
            dve.wait_ge(stat_link, base + 3)
            nc.vector.scalar_tensor_tensor(dist[:], quarter(2), 1.0 * QUARTERS / L, dist_sq[:], ALU.mult, ALU.add)\
              .then_inc(stat_link, 1)
            dve.wait_ge(stat_link, base + 4)
            nc.vector.tensor_reduce(spread[:], dist[:].rearrange("p (c q) -> p c q", q=QUARTERS), AX.X, ALU.add)\
              .then_inc(stat_link, 1)

        def group_variance(dve, b):
            dve.wait_ge(averaged, 2 * b + 2)
            nc.vector.tensor_scalar(var_g[:], average[1], 1.0 / QUARTERS, EPS, ALU.mult, ALU.add)\
              .then_inc(average_taken, 1)

        def group_affine(dve, b):
            base = b * STAT_LINKS
            dve.wait_ge(root_ready, b + 1)
            nc.vector.reciprocal(rstd[:], root[:]).then_inc(stat_link, 1)
            dve.wait_ge(stat_link, base + 6)
            nc.vector.tensor_tensor(newton[:], rstd[:], rstd[:], ALU.mult).then_inc(stat_link, 1)
            dve.wait_ge(stat_link, base + 7)
            nc.vector.scalar_tensor_tensor(newton[:], newton[:], -0.5, var_g[:], ALU.mult, ALU.mult)\
              .then_inc(stat_link, 1)
            dve.wait_ge(stat_link, base + 8)
            nc.vector.scalar_tensor_tensor(rstd[:], newton[:], 1.5, rstd[:], ALU.add, ALU.mult).then_inc(stat_link, 1)
            dve.wait_ge(stat_link, base + 9)
            nc.vector.tensor_tensor(scale_c[:], rstd[:], gamma[:], ALU.mult).then_inc(affine_step, 1)
            dve.wait_ge(affine_step, b * 2 + 1)
            nc.vector.tensor_tensor(newton[:], mean_g[:], scale_c[:], ALU.mult).then_inc(affine_step, 1)
            dve.wait_ge(affine_step, b * 2 + 2)
            nc.vector.tensor_tensor(shift_c[:], beta[:], newton[:], ALU.subtract).then_inc(affine_ready, 1)

        def split_hi(dve, b, c):
            dve.wait_ge(xn_full_ready, b * CT + (c + 1))
            nc.vector.tensor_copy(xn[:, 0, c, :], tile_of(c)).then_inc(xn_hi_ready, 1)

        def v_out(dve, b, st, use, slot, first=False):
            dve.wait_ge(acc_filled, use + 1)
            if st == 0 and not first:
                dve.wait_ge(v_pair_loaded, b * PAIRS * 16)
            nc.vector.tensor_tensor(v_img[:, st, :], acc[:, slot, :], bias_v[:], ALU.add).then_inc(acc_free, 1)

        def pair_bias(dve, j):
            nc.vector.tensor_scalar(bias_pair[:].rearrange("p (k o) -> p k o", o=1), bias_qk[:, :, bass.ds(j, 1)], 1.0,
                                    None, ALU.mult).then_inc(pair_bias_ready, 1)

        def qk_lo(dve, n, i, slot, k):
            which, tc = QK_GROUPS[i]
            for m, (h, part, px) in enumerate(PIECES[i][k]):
                dve.wait_ge(qk_hi_ready, n * HI_PARTS + (sum(len(p) for g in PIECES[:i] for p in g)
                                                         + k * len(PIECES[i][0]) + m + 1))
                rows, others = slice(h * CH, (h + 1) * CH), slice((1 - h) * CH, (2 - h) * CH)
                hi = (k_stack if which else q_stack)[rows, h, px]
                lo = k_lo[tc * CH:(tc + 1) * CH, h, :] if which else q_stack[others, h, px]
                last = nc.vector.scalar_tensor_tensor(lo, acc[rows, slot, part], bias_pair[rows, which:which + 1],
                                                      hi.bitcast(F32), ALU.add, ALU.subtract)
            if k == 1:
                last.then_inc(acc_free, 1)
            elif i >= 2:
                last.then_inc(q_piece_ready, 1)

        def q_hi_twice(dve, i, k):
            for h, _, px in PIECES[i][k]:
                rows, others = slice(h * CH, (h + 1) * CH), slice((1 - h) * CH, (2 - h) * CH)
                nc.vector.tensor_copy(q_other[others, px], q_stack[rows, h, px].bitcast(F32)).then_inc(q_other_ready, 1)

        def row_max(dve, g, i):
            dve.wait_ge(scores_ready, g * ITEMS + (i + 1))
            nc.vector.tensor_reduce(neg_max[:, i:i + 1], scores[:, i % 2, :], AX.X, ALU.max, negate=True)\
              .then_inc(max_ready, 1)

        def divide(dve, g, i):
            dve.wait_ge(exp_done, g * ITEMS + (i + 1))
            nc.vector.reciprocal(row_inv[:, i:i + 1], row_sum[:, i:i + 1]).then_inc(inv_ready, 1)
            dve.wait_ge(inv_ready, g * ITEMS + (i + 1))
            nc.vector.tensor_scalar(probs[:, i % 2, :], probs[:, i % 2, :], row_inv[:, i:i + 1], None, ALU.mult)\
              .then_inc(probs_ready, 1)

        def first_items(dve, n, slot):
            qk_lo(dve, n, 2, slot, 0)
            q_hi_twice(dve, 2, 0)
            qk_lo(dve, n, 2, slot, 1)
            row_max(dve, n, 0)
            row_max(dve, n, 1)
            q_hi_twice(dve, 2, 1)
            divide(dve, n, 0)

        def attn_out(dve, j, c, base, use):
            dve.wait_ge(acc_filled, base + (use + 1))
            nc.vector.tensor_copy(attn[:, bass.ds(j * L + c * CQ, CQ)], acc[:, bank(use), 0:CQ]).then_inc(acc_free, 1)

        def split_attn_lo(dve, b, c):
            dve.wait_ge(attn_hi_ready, b * PAIRS + (c + 1))
            nc.vector.tensor_tensor(attn_split[:, 1, c, :], attn[:, c * L:(c + 1) * L],
                                    attn_split[:, 0, c, :].bitcast(F32), ALU.subtract).then_inc(attn_lo_ready, 1)

        def proj_out(dve, b, n, base, use):
            ot = n // TC
            dve.wait_ge(acc_filled, base + (use + 1))
            dve.wait_ge(resid_loaded[n % 2], (b * (PROJ_GROUPS // 2) + (n // 2 + 1)) * 16)
            dve.wait_ge(done_free[n % 2], (b * (PROJ_GROUPS // 2) + (n // 2 + 1)) * 16)
            nc.vector.scalar_tensor_tensor(done[:, n % 2, :], acc[:, bank(use), :], bias_o[:, ot:ot + 1],
                                           resid[:, n % 2, :], ALU.add, ALU.add).then_inc(acc_free, 1)

        def vector_step(dve, b, j, kind):
            g = b * PAIRS + j
            base = acc_base(b, j)
            for i in range(ITEMS - 2):
                row_max(dve, g, i + 2)
                divide(dve, g, i + 1)
                if i in (4, 6):
                    qk_lo(dve, g, 3, bank(USE_LAST_QK), i // 6)
                    q_hi_twice(dve, 3, i // 6)
                if i == 10 and kind != "end":
                    pair_bias(dve, j + 1 if kind == "middle" else 0)
                if i in (8, 12):
                    attn_out(dve, j, i // 4 - 2, base, use_chunk(kind, i // 4 - 2))
                if kind in TURNS and i in SPLIT_SLOTS:
                    if i == SPLIT_SLOTS[0]:
                        dve.wait_ge(acc_filled, base + (USE_LAST_QK + 1))
                    split_hi(dve, b + 1, SPLIT_SLOTS.index(i))
            divide(dve, g, ITEMS - 1)
            attn_out(dve, j, 2, base, use_chunk(kind, 2))
            if kind != "end":
                dve.wait_ge(pair_bias_ready, g + 2)
                for i in range(2):
                    for k in range(2):
                        qk_lo(dve, g + 1, i, bank(use_qk(kind, i)), k)
                first_items(dve, g + 1, bank(use_qk(kind, 2)))
            attn_out(dve, j, CHUNKS - 1, base, use_chunk(kind, CHUNKS - 1))
            if kind in TURNS:
                for st in range(ST):
                    v_out(dve, b + 1, st, base + use_v(st), bank(use_v(st)))
                    if st < PAIRS:
                        split_attn_lo(dve, b, st)
                    elif kind == "turn":
                        image_stats(dve, b + 2, st - PAIRS)
            elif kind == "end":
                for c in range(PAIRS):
                    split_attn_lo(dve, b, c)
            if kind == "turn":
                sum_of_means(dve, b + 2)
            if kind != "middle":
                for n in range(PROJ_GROUPS):
                    proj_out(dve, b, n, base, use_out(kind, n))
                    if kind == "turn" and n < 3:
                        (group_mean, group_variance, group_affine)[n](dve, b + 2)

        @block.vector
        def _(dve):
            for n in range(2 * CT):
                dve.wait_ge(first_x_loaded[n // 2], 16)
                channel_stats(dve, n)
            sum_of_means(dve, 0)
            group_mean(dve, 0)
            group_variance(dve, 0)
            split_lo_weights(dve, w_raw[:, :, 2 * C:3 * C], w_v[:, 0, :, :], w_v[:, 1, :, :], 1.0, 1)
            dve.wait_ge(group_loaded, 48)
            group_affine(dve, 0)
            for c in range(CT):
                split_hi(dve, 0, c)
            split_lo(dve, 0, range(CT // 2, CT))
            for which, scale in enumerate((QSCALE, 1.0)):
                split_lo_weights(dve, w_raw[:, :, which * C:(which + 1) * C], *split_parts[which], scale, 2 + which)
            split_lo_weights(dve, w_o_raw, w_o[:, 0, :, :], w_o[:, 1, :, :], 1.0, 4)
            dve.wait_ge(consts_loaded, 16 * 4)
            nc.vector.tensor_scalar(bias_qk[:, 0, :], bias_qkv[:, 0:CT], QSCALE, None, ALU.mult).then_inc(bias_ready, 1)
            nc.vector.tensor_copy(bias_qk[:, 1, :], bias_qkv[:, CT:2 * CT]).then_inc(bias_ready, 1)
            dve.wait_ge(bias_ready, 2)
            pair_bias(dve, 0)
            for st in range(ST):
                v_out(dve, 0, st, st, st % 2, first=True)
                if st >= PAIRS:
                    image_stats(dve, 1, st - PAIRS)
            sum_of_means(dve, 1)
            dve.wait_ge(pair_bias_ready, 1)
            for i in range(2):
                for k in range(2):
                    qk_lo(dve, 0, i, i % 2, k)
                (group_mean, group_variance)[i](dve, 1)
            first_items(dve, 0, 0)
            group_affine(dve, 1)

            with dve.Fori(0, B - 2) as b:
                with dve.Fori(0, PAIRS - 1) as j:
                    vector_step(dve, b, j, "middle")
                vector_step(dve, b, PAIRS - 1, "turn")
            for b, kind in ((B - 2, "last turn"), (B - 1, "end")):
                with dve.Fori(0, PAIRS - 1) as j:
                    vector_step(dve, b, j, "middle")
                vector_step(dve, b, PAIRS - 1, kind)

        def bank_free(pe, use):
            pe.wait_ge(acc_free, use - 1)

        def group_average(pe, b, which):
            pe.wait_ge(stat_link, b * STAT_LINKS + (1, 5)[which])
            nc.tensor.matmul(average[which], group[:], (sum_means, spread)[which][:],
                             start=True, stop=True).then_inc(averaged, 1)

        def split_product(terms, out_ap, part=slice(None)):
            for n in range(len(terms))[part]:
                last = nc.tensor.matmul(out_ap, *terms[n], start=n == 0, stop=n == len(terms) - 1)
            return last

        def project_v(pe, st, use, slot, first=False):
            px = slice(st * P, (st + 1) * P)
            if not (first and st < 2):
                bank_free(pe, use)
            split_product([(xn[:, a, c, px], w_v[:, w, c, :]) for c in range(CT) for a, w in ((0, 0), (0, 1), (1, 0))],
                          acc[:, slot, :]).then_inc(acc_filled, 1)

        def project_qk(pe, i, use, slot, part=0, parts=1):
            which, tc = QK_GROUPS[i]
            if part == 0:
                bank_free(pe, use)
            terms = [(w_qk[:, w, c, which, :], xn[:, a, c, half(tc)])
                     for c in range(CT) for w, a in ((0, 0), (0, 1), (1, 0))]
            n = len(terms) // parts
            last = split_product(terms, acc[:, slot, :], slice(part * n, (part + 1) * n))
            if part == parts - 1:
                last.then_inc(acc_filled, 1)

        def score(pe, g, i, first=False):
            t, h = divmod(i, 2)
            if not first:
                pe.wait_ge(exp_done, g * ITEMS + (i - 1))
            lhs = q_stack[:, h, t * P:(t + 1) * P]
            for tc in range(TC):
                nc.tensor.matmul(scores[:, i % 2, half(tc)], lhs, k_stack[:, h, half(tc)], start=True, stop=False)
            if t % 2 == 0:
                pe.wait_ge(q_other_ready, g * 8 + (t + h + 1))
            for tc in range(TC):
                rows = slice(tc * CH, (tc + 1) * CH)
                q_hi = q_stack[rows, h, t * P:(t + 1) * P] if tc == h else q_other[rows, t * P:(t + 1) * P]
                last = nc.tensor.matmul(scores[:, i % 2, half(tc)], q_hi, k_lo[rows, h, :], start=False, stop=True)
            last.then_inc(scores_ready, 1)

        def transpose(pe, g, i):
            pe.wait_ge(probs_ready, g * ITEMS + (i + 1))
            for k in range(2):
                if i:
                    pe.wait_ge(probs_t_ready, g * 2 * ITEMS + (2 * i - 1 + k))
                for n in range(4):
                    s = (4 * k + n) * P
                    last = nc.tensor.transpose(turned[:, k, n, :], probs[:, i % 2, s:s + P], ident[:])
                last.then_inc(transposed, 1)

        def attend(pe, g, c, tiles, use, slot):
            if 0 in tiles:
                pe.wait_ge(probs_t_ready, g * 2 * ITEMS + 8 * (c + 1))
                if c == 0:
                    pe.wait_ge(v_pair_loaded, (g + 1) * 16)
                bank_free(pe, use)
            for st in tiles:
                for h in range(2):
                    rows = slice(h * CH, (h + 1) * CH)
                    last = nc.tensor.matmul(acc[rows, slot, 0:CQ], v_pair[:, st, rows], probs_t[:, c % 2, h, st, :],
                                            start=st == 0, stop=st == ST - 1)
            if ST - 1 in tiles:
                last.then_inc(acc_filled, 1)

        def project_out(pe, b, n, use, slot):
            ot, tc = divmod(n, TC)
            bank_free(pe, use)
            terms = [(w_o[:, w, c, ot * P:(ot + 1) * P], attn_split[:, a, c, half(tc)])
                     for c in range(CT) for w, a in ((0, 0), (0, 1), (1, 0))]
            for c in range(CT):
                if n == 0:
                    pe.wait_ge(attn_lo_ready, b * PAIRS + (c + 1))
                last = split_product(terms, acc[:, slot, :], slice(3 * c, 3 * (c + 1)))
            last.then_inc(acc_filled, 1)

        def tensor_step(pe, b, j, kind):
            g = b * PAIRS + j
            base = acc_base(b, j)
            spread_chunks = {4 * c + 4 + q: (c, range(2 * q, 2 * q + 2)) for c in range(2) for q in range(4)}
            spread_chunks.update({12: (2, range(0, 4)), 13: (2, range(4, 8))})
            for i in range(ITEMS - 2):
                if i + 2 == 4:
                    pe.wait_ge(acc_free, base)
                elif i + 2 == 8:
                    pe.wait_ge(q_piece_ready, g * 2 + 2)
                elif i + 2 == 12:
                    pe.wait_ge(acc_free, base + (USE_LAST_QK + 1))
                score(pe, g, i + 2)
                if i < 4:
                    project_qk(pe, 3, base + USE_LAST_QK, bank(USE_LAST_QK), i, 4)
                transpose(pe, g, i)
                if i in spread_chunks:
                    c, tiles = spread_chunks[i]
                    attend(pe, g, c, tiles, base + use_chunk(kind, c), bank(use_chunk(kind, c)))
            last_chunk = use_chunk(kind, CHUNKS - 1)
            if kind == "end":
                transpose(pe, g, ITEMS - 2)
                transpose(pe, g, ITEMS - 1)
                attend(pe, g, CHUNKS - 1, range(ST), base + last_chunk, bank(last_chunk))
            else:
                pe.wait_ge(w_qk_loaded, (g + 2) * 16)
                if kind in TURNS:
                    pe.wait_ge(xn_ready, (b + 2) * CT)
                for i in range(3):
                    project_qk(pe, i, base + use_qk(kind, i), bank(use_qk(kind, i)))
                    if i < 2:
                        transpose(pe, g, ITEMS - 2 + i)
                attend(pe, g, CHUNKS - 1, range(0, 4), base + last_chunk, bank(last_chunk))
                pe.wait_ge(q_piece_ready, (g + 1) * 2 + 1)
                score(pe, g + 1, 0)
                score(pe, g + 1, 1)
                attend(pe, g, CHUNKS - 1, range(4, ST), base + last_chunk, bank(last_chunk))
            if kind in TURNS:
                for st in range(ST):
                    project_v(pe, st, base + use_v(st), bank(use_v(st)))
            if kind != "middle":
                for n in range(PROJ_GROUPS):
                    use = use_out(kind, n)
                    project_out(pe, b, n, base + use, bank(use))
                    if kind == "turn" and n in (0, 2):
                        group_average(pe, b + 2, n // 2)
            if kind == "turn":
                pe.wait_ge(average_taken, 2 * (b + 2) + 2)

        @block.tensor
        def _(pe):
            pe.wait_ge(group_loaded, 48)
            group_average(pe, 0, 0)
            group_average(pe, 0, 1)
            pe.wait_ge(w_lo_ready, 1)
            pe.wait_ge(xn_ready, CT)
            for st in range(ST):
                project_v(pe, st, st, st % 2, first=True)
            pe.wait_ge(w_qk_loaded, 16)
            pe.wait_ge(consts_loaded, 16 * 4)
            for i in range(3):
                project_qk(pe, i, ST + i, i % 2)
                if i < 2:
                    group_average(pe, 1, i)
            pe.wait_ge(q_piece_ready, 1)
            score(pe, 0, 0, first=True)
            score(pe, 0, 1, first=True)
            pe.wait_ge(average_taken, 4)

            with pe.Fori(0, B - 2) as b:
                with pe.Fori(0, PAIRS - 1) as j:
                    tensor_step(pe, b, j, "middle")
                tensor_step(pe, b, PAIRS - 1, "turn")
            for b, kind in ((B - 2, "last turn"), (B - 1, "end")):
                with pe.Fori(0, PAIRS - 1) as j:
                    tensor_step(pe, b, j, "middle")
                tensor_step(pe, b, PAIRS - 1, kind)

    return nc


def kernel(x, L0_conv_gn_w, L0_conv_gn_b, L0_conv_qkv_w, L0_conv_qkv_b, L0_conv_proj_w, L0_conv_proj_b):
    import numpy as np
    import concourse.bacc as bacc
    from concourse.bass_utils import run_bass_kernel_spmd

    def columns(a):
        return np.ascontiguousarray(np.asarray(a).reshape(-1, P).T)

    same_group = np.arange(P)[:, None] // (C // GROUPS) == np.arange(P)[None, :] // (C // GROUPS)
    arrays = {
        "x": np.ascontiguousarray(np.asarray(x).reshape(B, C, L)),
        "w_qkv_t": np.ascontiguousarray(np.asarray(L0_conv_qkv_w).T),
        "w_proj_t": np.ascontiguousarray(np.asarray(L0_conv_proj_w).T),
        "b_qkv": columns(L0_conv_qkv_b),
        "b_v_row": np.ascontiguousarray(np.broadcast_to(np.asarray(L0_conv_qkv_b)[None, 2 * C:], (P, C))),
        "b_proj": columns(L0_conv_proj_b),
        "gn_w": columns(L0_conv_gn_w),
        "gn_b": columns(L0_conv_gn_b),
        "identity": np.eye(P, dtype=np.float32),
        "group_mean": same_group.astype(np.float32) / np.float32(C // GROUPS),
    }
    nc = bacc.Bacc("TRN2", target_bir_lowering=False, num_devices=1)
    args = [nc.dram_tensor(n, a.shape, F32, kind="ExternalInput").ap() for n, a in arrays.items()]
    out = nc.dram_tensor("out", (B, C, L), F32, kind="ExternalOutput").ap()
    build(nc, *args, out)
    result = run_bass_kernel_spmd(nc, [arrays], core_ids=[0])
    return result.results[0]["out"].reshape(B, C, 32, 32)
```
